# Optimizing a Trainium2 kernel written in Bass

```python
import numpy as np
import jax
import jax.numpy as jnp

def _softmax(x, axis=-1):
    return jax.nn.softmax(x, axis=axis)

def _gelu(x):
    return jax.nn.gelu(x, approximate=True)

def _silu(x):
    return jax.nn.silu(x)

def _sigmoid(x):
    return jax.nn.sigmoid(x)

def _layernorm(x, axis=-1, eps=1e-05):
    m = jnp.mean(x, axis=axis, keepdims=True)
    v = jnp.var(x, axis=axis, keepdims=True)
    return (x - m) / jnp.sqrt(v + eps)

def _scatter_add(tgt, idx, src, axis=0):
    return tgt.at[idx].add(src)

def _segment_sum(src, seg, n):
    return jax.ops.segment_sum(src, seg, n)
kernel_name = 'mk_decoder_preln_d1_seqx_r8_529eca'

def setup_inputs(seed: int=0):
    np.random.seed(seed)
    _w = jnp.asarray

    def _rec_inputs():
        import jax
        import jax.numpy as jnp
        _rk = jax.random.key(seed)
        x = 7.22e-05 + 1 * jax.random.normal(jax.random.fold_in(_rk, 1), (4, 256, 128), jnp.float32)
        _lenS = 256 - jax.random.randint(jax.random.fold_in(_rk, 7), (4,), 0, max(1, 256 // 4) + 1, jnp.int32)
        _lenS2 = 1601 - jax.random.randint(jax.random.fold_in(_rk, 8), (4,), 0, max(1, 1601 // 4) + 1, jnp.int32)
        _ctx_1024P = jax.random.normal(jax.random.fold_in(_rk, 11), (4, 16, 128), jnp.float32)
        _ctx_1024c = jax.random.dirichlet(jax.random.fold_in(_rk, 511), 0.3 * jnp.ones((16,), jnp.float32), (4, 1601))
        _ctx_1024t = jnp.einsum('bsk,bkd->bsd', _ctx_1024c, _ctx_1024P)
        _ctx_1024t = _ctx_1024t * jax.lax.rsqrt(jnp.mean(jnp.square(_ctx_1024t)) + 1e-12) * 0.953939
        ctx_1024 = 4.13588e-05 + 0.999923 * (_ctx_1024t + 0.3 * jax.random.normal(jax.random.fold_in(_rk, 611), (4, 1601, 128), jnp.float32))
        return (x, ctx_1024)
    x, ctx_1024 = _rec_inputs()

    def _L0_attn_setup():
        import jax, jax.numpy as jnp
        import numpy as np
        N_HEAD = 16
        MIN_CTX = 32
        FULL_CTX = 128

        def _pruning_ratio(T):
            if T < MIN_CTX:
                return 1.0
            if T >= FULL_CTX:
                return 0.2
            progress = (T - MIN_CTX) / (FULL_CTX - MIN_CTX)
            return 0.5 - 0.3 * progress
        key = jax.random.key(seed)
        ks = jax.random.split(key, 3)
        B, T, C = (2, 256, 128)
        x = jax.random.normal(ks[0], (B, T, C), jnp.float32)
        w_attn = jax.random.normal(ks[1], (3 * C, C), jnp.float32) * 0.02
        b_attn = jnp.zeros((3 * C,), jnp.float32)
        w_proj = jax.random.normal(ks[2], (C, C), jnp.float32) * 0.02
        b_proj = jnp.zeros((C,), jnp.float32)
        return {'x': x, 'w_attn': w_attn, 'b_attn': b_attn, 'w_proj': w_proj, 'b_proj': b_proj}
    _L0_attn_all = _L0_attn_setup()
    _L0_attn_in = {k: v for k, v in _L0_attn_all.items() if k in ('w_attn', 'b_attn', 'w_proj', 'b_proj')}
    del _L0_attn_all

    def _L0_xattn_setup():
        import jax, jax.numpy as jnp
        import numpy as np
        D_MODEL = 128
        NUM_HEADS = 16
        D_K = D_MODEL // NUM_HEADS
        key = jax.random.key(seed)
        ks = jax.random.split(key, 11)
        B, S, D = (4, 256, D_MODEL)
        scale = 1.0 / np.sqrt(D)
        return {'Q': jax.random.normal(ks[0], (B, S, D), jnp.float32), 'K': jax.random.normal(ks[1], (B, S, D), jnp.float32), 'V': jax.random.normal(ks[2], (B, S, D), jnp.float32), 'Wq': jax.random.normal(ks[3], (D, D), jnp.float32) * scale, 'bq': jnp.zeros((D,), jnp.float32), 'Wk': jax.random.normal(ks[4], (D, D), jnp.float32) * scale, 'bk': jnp.zeros((D,), jnp.float32), 'Wv': jax.random.normal(ks[5], (D, D), jnp.float32) * scale, 'bv': jnp.zeros((D,), jnp.float32), 'Wo': jax.random.normal(ks[6], (D, D), jnp.float32) * scale, 'bo': jnp.zeros((D,), jnp.float32)}
    _L0_xattn_all = _L0_xattn_setup()
    _L0_xattn_in = {k: v for k, v in _L0_xattn_all.items() if k in ('Wq', 'bq', 'Wk', 'bk', 'Wv', 'bv', 'Wo', 'bo')}
    del _L0_xattn_all

    def _L0_ffn_setup():
        import jax, jax.numpy as jnp
        import numpy as np
        BEST_K = 2

        def _expert(xf, w1, w3, w2):
            return jax.nn.silu(xf @ w1) * (xf @ w3) @ w2
        key = jax.random.key(seed)
        ks = jax.random.split(key, 9)
        E, S_sh, D, H = (8, 2, 128, 64)
        B, S = (2, 256)
        w = lambda k, shape: jax.random.normal(k, shape, dtype=jnp.float32) * 0.02
        return {'x': jax.random.normal(ks[0], (B, S, D), dtype=jnp.float32), 'router_w': w(ks[1], (D, E)), 'router_b': jnp.zeros((E,), dtype=jnp.float32), 'routed_w1': w(ks[2], (E, D, H)), 'routed_w3': w(ks[3], (E, D, H)), 'routed_w2': w(ks[4], (E, H, D)), 'shared_w1': w(ks[5], (S_sh, D, H)), 'shared_w3': w(ks[6], (S_sh, D, H)), 'shared_w2': w(ks[7], (S_sh, H, D))}
    _L0_ffn_all = _L0_ffn_setup()
    _L0_ffn_in = {k: v for k, v in _L0_ffn_all.items() if k in ('router_w', 'router_b', 'routed_w1', 'routed_w3', 'routed_w2', 'shared_w1', 'shared_w3', 'shared_w2')}
    del _L0_ffn_all
    return {'x': x, 'ctx_1024': ctx_1024, 'L0_attn_w_attn': _L0_attn_in['w_attn'], 'L0_attn_b_attn': _L0_attn_in['b_attn'], 'L0_attn_w_proj': _L0_attn_in['w_proj'], 'L0_attn_b_proj': _L0_attn_in['b_proj'], 'L0_xattn_Wq': _L0_xattn_in['Wq'], 'L0_xattn_bq': _L0_xattn_in['bq'], 'L0_xattn_Wk': _L0_xattn_in['Wk'], 'L0_xattn_bk': _L0_xattn_in['bk'], 'L0_xattn_Wv': _L0_xattn_in['Wv'], 'L0_xattn_bv': _L0_xattn_in['bv'], 'L0_xattn_Wo': _L0_xattn_in['Wo'], 'L0_xattn_bo': _L0_xattn_in['bo'], 'L0_ffn_router_w': _L0_ffn_in['router_w'], 'L0_ffn_router_b': _L0_ffn_in['router_b'], 'L0_ffn_routed_w1': _L0_ffn_in['routed_w1'], 'L0_ffn_routed_w3': _L0_ffn_in['routed_w3'], 'L0_ffn_routed_w2': _L0_ffn_in['routed_w2'], 'L0_ffn_shared_w1': _L0_ffn_in['shared_w1'], 'L0_ffn_shared_w3': _L0_ffn_in['shared_w3'], 'L0_ffn_shared_w2': _L0_ffn_in['shared_w2']}

def reference(x, ctx_1024, L0_attn_w_attn, L0_attn_b_attn, L0_attn_w_proj, L0_attn_b_proj, L0_xattn_Wq, L0_xattn_bq, L0_xattn_Wk, L0_xattn_bk, L0_xattn_Wv, L0_xattn_bv, L0_xattn_Wo, L0_xattn_bo, L0_ffn_router_w, L0_ffn_router_b, L0_ffn_routed_w1, L0_ffn_routed_w3, L0_ffn_routed_w2, L0_ffn_shared_w1, L0_ffn_shared_w3, L0_ffn_shared_w2):
    import jax
    import jax.numpy as jnp

    def _L0_attn_ref(x, w_attn, b_attn, w_proj, b_proj):
        import jax, jax.numpy as jnp
        import numpy as np
        N_HEAD = 16
        MIN_CTX = 32
        FULL_CTX = 128

        def _pruning_ratio(T):
            if T < MIN_CTX:
                return 1.0
            if T >= FULL_CTX:
                return 0.2
            progress = (T - MIN_CTX) / (FULL_CTX - MIN_CTX)
            return 0.5 - 0.3 * progress
        B, T, C = x.shape
        nh = N_HEAD
        hd = C // nh
        neg_inf = jnp.float32(-jnp.inf)
        qkv = x @ w_attn.T + b_attn
        q, k, v = jnp.split(qkv, 3, axis=2)
        to_heads = lambda t: t.reshape(B, T, nh, hd).transpose(0, 2, 1, 3)
        q, k, v = (to_heads(q), to_heads(k), to_heads(v))
        att = jnp.einsum('bhid,bhjd->bhij', q, k) / jnp.sqrt(jnp.float32(hd))
        i = jnp.arange(T)
        causal = i[None, :] <= i[:, None]
        att = jnp.where(causal[None, None], att, neg_inf)
        S = jax.nn.relu(att[:, 0])
        S = S.at[..., 0].set(0.0)
        S = S * (1.0 - jnp.eye(T, dtype=S.dtype))
        S_shifted = jnp.concatenate([jnp.zeros((B, 1, T), S.dtype), S[:, :-1]], axis=1)
        FF = jnp.cumsum(S_shifted, axis=1)
        att = att - FF[:, None]
        ratio = _pruning_ratio(T)
        memory_budget = max(1, int(T * ratio))
        if ratio < 1.0:
            FF_mod = jnp.where(causal[None], FF, jnp.inf)
            sorted_idx = jnp.argsort(FF_mod, axis=-1)
            rank = jnp.argsort(sorted_idx, axis=-1)
            eff_k = jnp.minimum(memory_budget - 1, i + 1)
            keep = rank < eff_k[None, :, None]
            keep = keep | jnp.eye(T, dtype=bool)[None]
            att = jnp.where(keep[:, None], att, neg_inf)
        y = jax.nn.softmax(att, axis=-1) @ v
        y = y.transpose(0, 2, 1, 3).reshape(B, T, C)
        return y @ w_proj.T + b_proj

    def _L0_xattn_ref(Q, K, V, Wq, bq, Wk, bk, Wv, bv, Wo, bo):
        import jax, jax.numpy as jnp
        import numpy as np
        D_MODEL = 128
        NUM_HEADS = 16
        D_K = D_MODEL // NUM_HEADS
        B, S, D = Q.shape
        H, Dk = (NUM_HEADS, D_K)

        def proj(x, W, b):
            y = jnp.einsum('bsd,de->bse', x, W.T) + b
            return y.reshape(B, -1, H, Dk).transpose(0, 2, 1, 3)
        q = proj(Q, Wq, bq)
        k = proj(K, Wk, bk)
        v = proj(V, Wv, bv)
        scores = jnp.einsum('bhqd,bhkd->bhqk', q, k) / np.sqrt(Dk)
        attn = jax.nn.softmax(scores, axis=-1)
        out = jnp.einsum('bhqk,bhkd->bhqd', attn, v)
        out = out.transpose(0, 2, 1, 3).reshape(B, -1, D)
        return jnp.einsum('bsd,de->bse', out, Wo.T) + bo

    def _L0_ffn_ref(x, router_w, router_b, routed_w1, routed_w3, routed_w2, shared_w1, shared_w3, shared_w2):
        import jax, jax.numpy as jnp
        import numpy as np
        BEST_K = 2

        def _expert(xf, w1, w3, w2):
            return jax.nn.silu(xf @ w1) * (xf @ w3) @ w2
        B, S, D = x.shape
        T = B * S
        xf = x.reshape(T, D)
        logits = xf @ router_w + router_b
        topk_vals, topk_idx = jax.lax.top_k(logits, BEST_K)
        sparse = jnp.full_like(logits, -jnp.inf)
        sparse = sparse.at[jnp.arange(T)[:, None], topk_idx].set(topk_vals)
        gates = jax.nn.softmax(sparse, axis=-1)
        routed = jax.vmap(_expert, in_axes=(None, 0, 0, 0))(xf, routed_w1, routed_w3, routed_w2)
        routed_out = jnp.einsum('etd,te->td', routed, gates)
        shared_out = jax.vmap(_expert, in_axes=(None, 0, 0, 0))(xf, shared_w1, shared_w3, shared_w2).sum(axis=0)
        return (routed_out + shared_out).reshape(B, S, D)
    x = x + _L0_attn_ref(_layernorm(x, axis=-1), L0_attn_w_attn, L0_attn_b_attn, L0_attn_w_proj, L0_attn_b_proj)
    x = x + _L0_xattn_ref(_layernorm(x, axis=-1), ctx_1024, ctx_1024, L0_xattn_Wq, L0_xattn_bq, L0_xattn_Wk, L0_xattn_bk, L0_xattn_Wv, L0_xattn_bv, L0_xattn_Wo, L0_xattn_bo)
    x = x + _L0_ffn_ref(_layernorm(x, axis=-1), L0_ffn_router_w, L0_ffn_router_b, L0_ffn_routed_w1, L0_ffn_routed_w3, L0_ffn_routed_w2, L0_ffn_shared_w1, L0_ffn_shared_w3, L0_ffn_shared_w2)
    return x

_drawn_inputs = setup_inputs


def setup_inputs(seed=0):
    import zlib

    import numpy as np

    out = dict(_drawn_inputs(seed))
    spreads = {'L0_attn_b_attn': (0.0, 0.45),
     'L0_attn_b_proj': (0.0, 0.1),
     'L0_xattn_bq': (0.0, 0.375),
     'L0_xattn_bk': (0.0, 0.8),
     'L0_xattn_bv': (0.0, 0.1),
     'L0_xattn_bo': (0.0, 0.1),
     'L0_ffn_router_b': (0.0, 0.8)}
    factors = {'L0_attn_w_attn': 6.407,
     'L0_attn_w_proj': 2.879,
     'L0_ffn_router_w': 8.0,
     'L0_ffn_routed_w1': 8.0,
     'L0_ffn_routed_w3': 8.0,
     'L0_ffn_routed_w2': 8.0,
     'L0_ffn_shared_w1': 8.0,
     'L0_ffn_shared_w3': 8.0,
     'L0_ffn_shared_w2': 8.0}
    for name, (base, spread) in spreads.items():
        noise = np.random.default_rng([zlib.crc32(name.encode()), seed]).standard_normal(out[name].shape)
        drawn = base * np.exp(spread * noise) if base else spread * noise
        out[name] = jnp.asarray(drawn.astype(out[name].dtype))
    for name, factor in factors.items():
        out[name] = (out[name] * factor).astype(out[name].dtype)
    return out
```

```python
from contextlib import ExitStack

import numpy as np

import concourse.bass as bass
from concourse import mybir

F32 = mybir.dt.float32
BF16 = mybir.dt.bfloat16
ALU = mybir.AluOpType
ACT = mybir.ActivationFunctionType
AX = mybir.AxisListType

B, T, C, S = 4, 256, 128, 1601
H = 16
D = C // H
P = 128
NT = T // P
NC = -(-S // P)
LAST = S - (NC - 1) * P
G = 4
HG = H // G
NP = H // 2
E_RT, E_SH, HID = 8, 2, 64
NB = (E_RT + E_SH) * HID // P
NB_RT = E_RT * HID // P
KEEP = 50
ROUNDS = 7
DUMMY = ROUNDS * 8 - KEEP
TOP = 2
GDUMMY = 8 - TOP
SCALE = float(1.0 / np.sqrt(np.float32(D)))
EPS = 1e-5
BIG = 1.0e30
TAKEN = -3.0e38
TAKEN_BELOW = -2.0e38

PARTS = 6
HEAD_ROWS = PARTS * D
QK_ROWS = 2 * HEAD_ROWS
ALL_ROWS = QK_ROWS + 2

W_QKV, W_PROJ, W_XQ, W_XK, W_XV, W_XO = 0, 3 * C, 4 * C, 5 * C, 6 * C, 7 * C
W_R = 8 * C
W_1 = W_R + E_RT
W_3 = W_1 + NB * P
W_2 = W_3 + NB * P
W_ALL = W_2 + NB * P
B_Q, B_XQ, B_K, B_XK = range(4)
R_V, R_PROJ, R_XV, R_XO, R_R = 0, C, 2 * C, 3 * C, 4 * C
R_ALL = 4 * C + E_RT

PIECES = [(0, 401), (401, 400), (801, 400), (1201, 400)]
KBANKS = [(0, 512), (512, 512), (1024, 512), (1536, S - 1536)]
VGROUPS = [range(0, 4), range(4, 8), range(8, 12), range(12, 13)]



class Stage:

    def __init__(self, sem, per):
        self.sem, self.per = sem, per

    def now(self, b, n=None):
        return b * self.per + (self.per if n is None else n)

    def last(self, b, n=None):
        return (b - 1) * self.per + (self.per if n is None else n)


def wait_past(eng, sem, value):
    if value > 0:
        eng.wait_ge(sem, value)


class Slots:

    def __init__(self, full, empty, jobs):
        n = len(full)
        self.jobs, self.n = jobs, n
        self.index = {job: i for i, job in enumerate(jobs)}
        uses = [len(range(k, len(jobs), n)) for k in range(n)]
        self.full = [Stage(s, u) for s, u in zip(full, uses)]
        self.empty = [Stage(s, u) for s, u in zip(empty, uses)]
        assert len(self.index) == len(jobs)

    def at(self, job):
        return self.index[job] % self.n

    def use(self, job):
        return self.index[job] // self.n + 1

    def filled(self, job):
        return self.full[self.at(job)].sem

    def emptied(self, job):
        return self.empty[self.at(job)].sem

    def wait_filled(self, eng, job, b):
        s = self.full[self.at(job)]
        eng.wait_ge(s.sem, s.now(b, self.use(job)))

    def wait_emptied(self, eng, job, b):
        s = self.empty[self.at(job)]
        eng.wait_ge(s.sem, s.now(b, self.use(job)))

    def wait_free(self, eng, job, b):
        s = self.empty[self.at(job)]
        wait_past(eng, s.sem, s.now(b, self.use(job) - 1))


def build(nc, x, ctxT, w_all, col_bias, row_bias, out):
    with ExitStack() as ctx:
        def sb(name, shape, dt=F32):
            return ctx.enter_context(nc.sbuf_tensor(name, shape, dt))

        def ps(name, shape):
            return ctx.enter_context(nc.psum_tensor(name, shape, F32))

        def sem(name):
            return ctx.enter_context(nc.semaphore(name))

        w = sb("w", [P, W_ALL])
        colb = sb("colb", [P, 4])
        colbs = sb("colbs", [P, 2])
        rowb = sb("rowb", [P, R_ALL])
        ident = sb("ident", [P, P])
        neg_before = sb("neg_before", [P, P])
        neg_ones = sb("neg_ones", [P, P])
        earlier = sb("earlier", [P, NT, T])
        acausal = sb("acausal", [P, NT, T])
        off_diag = sb("off_diag", [P, NT, T])
        minus_half = sb("minus_half", [P, NT, 1])
        expert_rows = sb("expert_rows", [E_RT, NB_RT, P])
        xin = sb("xin", [P, NT, C])
        xb = sb("xb", [P, NT, C])
        ctx_sb = sb("ctx_sb", [P, S])
        stats = sb("stats", [P, NT, 6])
        mv = sb("mv", [P, NT, 2])
        rstd = sb("rstd", [P, NT, 1])
        var_eps = sb("var_eps", [P, NT, 1])
        xn = sb("xn", [P, NT, C])
        xnT = sb("xnT", [P, T])
        qk = sb("qk", [P, 2, T])
        qk_rest = sb("qk_rest", [P, 2, T])
        qk_part = sb("qk_part", [P, 3, 2, T], BF16)
        Qs = sb("Qs", [P, NP, 2, T], BF16)
        Ks = sb("Ks", [P, NP, T], BF16)
        Vs = sb("Vs", [P, NT, H, 32])
        S0 = sb("S0", [P, NT, T])
        nff = sb("nff", [P, NT, T + DUMMY])
        top = sb("top", [P, 2, NT, T + DUMMY])
        top8 = sb("top8", [P, NT, 8])
        drop = sb("drop", [P, NT, T])
        bias = sb("bias", [P, NT, T])
        biasT = sb("biasT", [P, 3 * P])
        junk = sb("junk", [P, 2, NT, T])
        smax = sb("smax", [P, NT, H])
        sm_neg = sb("sm_neg", [H, T])
        sm_part = sb("sm_part", [H, 2, T], BF16)
        biased = sb("biased", [P, 2, HG * T])
        probs = sb("probs", [P, 3, HG * T])
        yT = sb("yT", [P, G, T])
        rden = sb("rden", [P, NT, H])
        yrow = sb("yrow", [P, NT, C])
        ycT = sb("ycT", [P, T])
        x1 = sb("x1", [P, NT, C])
        x1b = sb("x1b", [P, NT, C])
        kf = sb("kf", [P, S])
        k_rest = sb("k_rest", [P, S])
        k_part = sb("k_part", [P, 3, S], BF16)
        Kx = sb("Kx", [P, NP, S], BF16)
        Qx = sb("Qx", [P, NP, 2, T], BF16)
        Vx = sb("Vx", [P, NC, H, 32])
        xmax4 = sb("xmax4", [P, 2, NT, HG, 4])
        xmax = sb("xmax", [P, 2, NT, HG])
        xm_neg = sb("xm_neg", [HG, T])
        xm_part = sb("xm_part", [HG, 2, 2, T], BF16)
        x2 = sb("x2", [P, NT, C])
        logits = sb("logits", [P, NT, E_RT + GDUMMY])
        ranked = sb("ranked", [P, NT, E_RT + GDUMMY])
        best8 = sb("best8", [P, NT, 8])
        neg_best = sb("neg_best", [P, NT, 1])
        eg = sb("eg", [P, NT, E_RT])
        egm = sb("egm", [P, NT, E_RT])
        gates = sb("gates", [P, NT, E_RT])
        gsum = sb("gsum", [P, NT, 1])
        grec = sb("grec", [P, NT, 1])
        gatesT = sb("gatesT", [E_RT, T])
        en = sb("en", [P, 2, T])
        en1 = sb("en1", [P, 2, T])
        sg = sb("sg", [P, 2, T])
        hs = sb("hs", [P, 2, T])
        hu = sb("hu", [P, 2, T])
        hT = sb("hT", [P, NB, T])
        xout = sb("xout", [P, NT, C])

        scr_q = nc.dram_tensor("scr_q", (H, D, 6, T), BF16, kind="Internal").ap()
        scr_k = nc.dram_tensor("scr_k", (H, D, 6, T), BF16, kind="Internal").ap()
        scr_xk = nc.dram_tensor("scr_xk", (H, D, 6, S), BF16, kind="Internal").ap()

        p_sc = [ps(f"p_sc{i}", [P, 2, 512]) for i in range(2)]
        p_pv = ps("p_pv", [P, 512])
        p_r = [ps(f"p_r{i}", [P, 512]) for i in range(3)]

        pieces = [("xmax", g, t, j, n) for g in range(G) for t in range(NT) for j in range(HG)
                  for n in range(len(PIECES))]
        PG = len(pieces) // G
        LEAD, TURN = PG + 20, 4
        cross = []
        sent = 0

        def pieces_to(n):
            nonlocal sent
            while sent < min(n, len(pieces)):
                cross.append(pieces[sent])
                sent += 1
                if sent % PG == 0:
                    cross.append(("xmax8", pieces[sent - 1][1]))
                if sent >= PG + TURN and (sent - TURN) % PG == 0:
                    cross.append(("xmT", (sent - TURN) // PG - 1))
                if sent == len(pieces):
                    cross.append(("xmT", G - 1))

        pieces_to(LEAD)
        for i in range(G * NC):
            cross.append(("score", *divmod(i, NC)))
            pieces_to(LEAD + (PG * (i + 1)) // NC)
            if i:
                cross.append(("sum", *divmod(i - 1, NC)))
        cross.append(("sum", G - 1, NC - 1))

        ring_jobs = ["xn1T", "qk", "v"]
        ring_jobs += [("k", n) for n in range(4)] + [("vx", n) for n in range(4)]
        ring_jobs += ["score0", "ff", "biasT"]
        ring_jobs += [("smax", h) for h in range(H)] + ["smT"]
        ring_jobs += [("sy", t) for t in range(NT)] + ["sycT", "sproj", "xn2T", "q2"]
        ring_jobs += [step for step in cross if step[0] in ("xmax", "xmT")]
        ring_jobs += [("xy", t) for t in range(NT)] + ["xycT", "xproj", "xn3T", "router", "gatesT"]
        for n in range(NB):
            ring_jobs += [("h13", n)] + ([("gate", n)] if n < NB_RT else [])
        ring_jobs += ["ffn"]
        exp_jobs = [("s", g, t) for g in range(G) for t in range(NT)]
        exp_jobs += [("x", g, c) for g in range(G) for c in range(NC)]

        stages = []

        def stage(name, per):
            stages.append(Stage(sem(name), per))
            return stages[-1]

        def slots(name, n, jobs):
            made = Slots([sem(f"{name}_filled{i}") for i in range(n)],
                         [sem(f"{name}_emptied{i}") for i in range(n)], jobs)
            stages.extend(made.full + made.empty)
            return made

        def wait_scores_taken(eng, job, b):
            i = exp_jobs.index(job) - len(p_sc)
            before = exp_jobs[i]
            taken = sc if before[0] == "s" else pr
            s = (taken.empty if before[0] == "s" else taken.full)[taken.at(before)]
            wait_past(eng, s.sem, s.now(b, taken.use(before)) if i >= 0 else s.last(b, taken.use(before)))

        ring = slots("ring", 3, ring_jobs)
        sc = slots("scores", 2, exp_jobs)
        for s in sc.empty:
            s.per = G * NT // 2
        pr = slots("probs", 3, exp_jobs)
        sums_kept = stage("sums_kept", 2 * G)

        w_in, rows_set, const_step, consts, colbs_ready = sem("w_in"), sem("rows_set"), sem("const_step"), sem("consts"), sem("colbs_ready")
        x_in, ctx_in = stage("x_in", 16), stage("ctx_in", 16)
        ln_step, xn_ready = stage("ln_step", 12), stage("xn_ready", 6)
        var_ready, rstd_ready = stage("var_ready", 3), stage("rstd_ready", 3)
        part_step, part_ready = stage("part_step", 6), stage("part_ready", 2)
        sqk_written, sqk_packed = stage("sqk_written", 96), stage("sqk_packed", 48)
        q2_written, q2_packed = stage("q2_written", 48), stage("q2_packed", 32)
        top_step = stage("top_step", 4 * ROUNDS)
        drop_ready, bias_ready = stage("drop_ready", 1), stage("bias_ready", 1)
        smax_first = stage("smax_first", H)
        sm_step, sm_ready, sm_packed = stage("sm_step", 1), stage("sm_ready", 1), stage("sm_packed", 32)
        rden_ready = stage("rden_ready", 4)
        xb_ready, x1b_ready = stage("xb_ready", 1), stage("x1b_ready", 1)
        kpart_step, kpart_ready = stage("kpart_step", 3), stage("kpart_ready", 1)
        xk_written, xk_packed = stage("xk_written", 48), stage("xk_packed", 16 * G)
        xmax_ready = stage("xmax_ready", G)
        xm_step, xm_ready, xm_packed = stage("xm_step", G), stage("xm_ready", G), stage("xm_packed", 32 * G)
        gate_step, eg_ready, gates_ready = stage("gate_step", 8), stage("eg_ready", 2), stage("gates_ready", 1)
        en_ready, en1_ready = stage("en_ready", NB), stage("en1_ready", NB)
        h_step = stage("h_step", 2 * NB)
        stored = stage("stored", 16)

        block = ctx.enter_context(nc.Block())

        @block.sync
        def _(sp):
            sp.dma_start(w[:], w_all).then_inc(w_in, 16)
            sp.dma_start(colb[:], col_bias).then_inc(w_in, 16)
            sp.dma_start(rowb[:], row_bias.to_broadcast([P, R_ALL])).then_inc(w_in, 16)
            sp.wait_ge(rows_set, 3)

            def to_scratch(scratch, src, repeat, done):
                dst = scratch.rearrange("h d c n -> (h d) c n")
                n = src.shape[-1]
                for k, (c0, width) in enumerate(((0, 3), (3, 2), (5, 1))):
                    part = src[:, k:k + 1, :].to_broadcast([P, width, n]) if repeat else src[:, 0:width, :]
                    sp.dma_start(dst[:, c0:c0 + width, :], part).then_inc(done.sem, 16)

            def keys_from_scratch(dst, scratch, p0, p1, done):
                src = scratch.rearrange("(p s) d c n -> (s d c) p n", s=2)
                sp.dma_start(dst[0:QK_ROWS, p0:p1, :], src[:, p0:p1, :]).then_inc(done.sem, 16)

            def queries_from_scratch(dst, scratch, done):
                src = scratch.rearrange("(p s) d c n -> s (d c) p n", s=2)
                for s in range(2):
                    sp.dma_start(dst[s * HEAD_ROWS:(s + 1) * HEAD_ROWS, :, s, :], src[s]).then_inc(done.sem, 16)

            def max_rows(dst, part, p0, p1, done):
                for r in range(2):
                    row = dst[QK_ROWS + r:QK_ROWS + r + 1, p0:p1].rearrange("o p s n -> o (p s) n")
                    sp.dma_start(row, part[:, r, :]).then_inc(done.sem, 16)

            for b in range(B):
                wait_past(sp, xn_ready.sem, xn_ready.last(b, 2))
                wait_past(sp, xb_ready.sem, xb_ready.last(b))
                sp.dma_start(xin[:], x[b].rearrange("(t p) c -> p t c", p=P)).then_inc(x_in.sem, 16)
                s = ring.full[ring.at(("vx", 3))]
                wait_past(sp, s.sem, s.last(b, ring.use(("vx", 3))))
                sp.dma_start(ctx_sb[:], ctxT[b]).then_inc(ctx_in.sem, 16)
                sp.wait_ge(part_ready.sem, part_ready.now(b, 1))
                to_scratch(scr_q, qk_part[:, :, 0, :], True, sqk_written)
                to_scratch(scr_k, qk_part[:, :, 1, :], False, sqk_written)
                sp.wait_ge(sqk_written.sem, sqk_written.now(b))
                queries_from_scratch(Qs, scr_q, sqk_packed)
                keys_from_scratch(Ks, scr_k, 0, NP, sqk_packed)
                sp.wait_ge(rows_set, 4)
                sp.wait_ge(kpart_ready.sem, kpart_ready.now(b))
                to_scratch(scr_xk, k_part[:], False, xk_written)
                sp.wait_ge(xk_written.sem, xk_written.now(b))
                for g in range(G):
                    keys_from_scratch(Kx, scr_xk, 2 * g, 2 * g + 2, xk_packed)
                sp.wait_ge(sm_ready.sem, sm_ready.now(b))
                max_rows(Qs, sm_part, 0, NP, sm_packed)
                sp.wait_ge(part_ready.sem, part_ready.now(b, 2))
                to_scratch(scr_q, qk_part[:, :, 0, :], True, q2_written)
                sp.wait_ge(q2_written.sem, q2_written.now(b))
                queries_from_scratch(Qx, scr_q, q2_packed)
                for g in range(G):
                    sp.wait_ge(xm_ready.sem, xm_ready.now(b, g + 1))
                    max_rows(Qx, xm_part[:, g % 2], 2 * g, 2 * g + 2, xm_packed)
                ring.wait_emptied(sp, "ffn", b)
                sp.dma_start(out[b].rearrange("(t p) c -> p t c", p=P), xout[:]).then_inc(stored.sem, 16)
            sp.wait_ge(stored.sem, stored.now(B - 1))

        @block.gpsimd
        def _(pool):
            count = [0]

            def step(ins):
                count[0] += 1
                ins.then_inc(const_step, 1)
                pool.wait_ge(const_step, count[0])

            nc.gpsimd.memset(ident[:], 0.0)
            nc.gpsimd.memset(neg_before[:], -1.0)
            nc.gpsimd.memset(neg_ones[:], -1.0)
            nc.gpsimd.memset(earlier[:], 1.0)
            nc.gpsimd.memset(acausal[:], 0.0)
            nc.gpsimd.memset(off_diag[:], -BIG)
            nc.gpsimd.memset(expert_rows[:], 1.0)
            nc.gpsimd.memset(Vs[:], 0.0)
            nc.gpsimd.memset(minus_half[:], -0.5)
            nc.gpsimd.memset(nff[:, :, T:], 1.0)
            nc.gpsimd.memset(logits[:, :, E_RT:], 3.0e38)
            step(nc.gpsimd.memset(Vx[:], 0.0))
            nc.gpsimd.memset(Vs[:, :, :, D:D + 1], 1.0)
            nc.gpsimd.memset(Vx[:, :, :, D:D + 1], 1.0)
            nc.gpsimd.affine_select(out=ident[:], in_=ident[:], compare_op=ALU.not_equal, fill=1.0, base=0,
                                    pattern=[[-1, P]], channel_multiplier=1)
            nc.gpsimd.affine_select(out=neg_before[:], in_=neg_before[:], compare_op=ALU.is_gt, fill=0.0, base=0,
                                    pattern=[[1, P]], channel_multiplier=-1)
            nc.gpsimd.affine_select(out=acausal[:], in_=acausal[:], compare_op=ALU.is_ge, fill=-BIG, base=0,
                                    pattern=[[P, NT], [-1, T]], channel_multiplier=1)
            nc.gpsimd.affine_select(out=off_diag[:], in_=off_diag[:], compare_op=ALU.not_equal, fill=0.0, base=0,
                                    pattern=[[P, NT], [-1, T]], channel_multiplier=1)
            step(nc.gpsimd.affine_select(out=earlier[:], in_=earlier[:], compare_op=ALU.is_gt, fill=0.0, base=0,
                                         pattern=[[P, NT], [-1, T]], channel_multiplier=1))
            nc.gpsimd.memset(earlier[:, :, 0:1], 0.0)
            step(nc.gpsimd.affine_select(out=expert_rows[:], in_=expert_rows[:], compare_op=ALU.is_ge, fill=0.0,
                                         base=0, pattern=[[P, NB_RT], [1, P]], channel_multiplier=-HID))
            nc.gpsimd.affine_select(out=expert_rows[:], in_=expert_rows[:], compare_op=ALU.is_ge, fill=0.0,
                                    base=HID - 1, pattern=[[-P, NB_RT], [-1, P]],
                                    channel_multiplier=HID).then_inc(consts, 1)
            pool.wait_ge(w_in, 48)

            def row(r0):
                return rowb[:, r0:r0 + C].unsqueeze(1).to_broadcast([P, NT, C])

            def inverse_std(k, b):
                pool.wait_ge(ln_step.sem, ln_step.now(b, 4 * k + 4))
                nc.gpsimd.tensor_scalar(var_eps[:], mv[:, :, 1:2], EPS, None, ALU.add).then_inc(var_ready.sem, 1)
                pool.wait_ge(var_ready.sem, var_ready.now(b, k + 1))
                nc.gpsimd.tensor_tensor(rstd[:], var_eps[:], minus_half[:], ALU.pow).then_inc(rstd_ready.sem, 1)

            for b in range(B):
                inverse_std(0, b)
                pool.wait_ge(x_in.sem, x_in.now(b))
                s = ring.empty[ring.at("sproj")]
                wait_past(pool, s.sem, s.last(b, ring.use("sproj")))
                nc.gpsimd.tensor_tensor(xb[:], xin[:], row(R_PROJ), ALU.add).then_inc(xb_ready.sem, 1)
                for n in range(1, 4):
                    ring.wait_emptied(pool, ("k", n), b)
                wait_past(pool, xk_written.sem, xk_written.last(b))
                nc.gpsimd.tensor_copy(k_part[:, 0, :], kf[:]).then_inc(kpart_step.sem, 1)
                pool.wait_ge(kpart_step.sem, kpart_step.now(b, 1))
                nc.gpsimd.tensor_tensor(k_rest[:], kf[:], k_part[:, 0, :], ALU.subtract).then_inc(kpart_step.sem, 1)
                pool.wait_ge(kpart_step.sem, kpart_step.now(b, 2))
                nc.gpsimd.tensor_copy(k_part[:, 1, :], k_rest[:]).then_inc(kpart_step.sem, 1)
                pool.wait_ge(kpart_step.sem, kpart_step.now(b, 3))
                nc.gpsimd.tensor_tensor(k_part[:, 2, :], k_rest[:], k_part[:, 1, :],
                                        ALU.subtract).then_inc(kpart_ready.sem, 1)
                ring.wait_emptied(pool, "smT", b)
                nc.gpsimd.tensor_copy(sm_part[:, 0, :], sm_neg[:]).then_inc(sm_step.sem, 1)
                pool.wait_ge(sm_step.sem, sm_step.now(b))
                nc.gpsimd.tensor_tensor(sm_part[:, 1, :], sm_neg[:], sm_part[:, 0, :],
                                        ALU.subtract).then_inc(sm_ready.sem, 1)
                inverse_std(1, b)
                ring.wait_emptied(pool, "sproj", b)
                nc.gpsimd.tensor_tensor(x1b[:], x1[:], row(R_XO), ALU.add).then_inc(x1b_ready.sem, 1)
                for g in range(G):
                    ring.wait_emptied(pool, ("xmT", g), b)
                    if g >= 2:
                        pool.wait_ge(xm_packed.sem, xm_packed.now(b, 32 * (g - 1)))
                    nc.gpsimd.tensor_copy(xm_part[:, g % 2, 0, :], xm_neg[:]).then_inc(xm_step.sem, 1)
                    pool.wait_ge(xm_step.sem, xm_step.now(b, g + 1))
                    nc.gpsimd.tensor_tensor(xm_part[:, g % 2, 1, :], xm_neg[:], xm_part[:, g % 2, 0, :],
                                            ALU.subtract).then_inc(xm_ready.sem, 1)
                inverse_std(2, b)
                for n in range(NB):
                    pool.wait_ge(en_ready.sem, en_ready.now(b, n + 1))
                    if n >= 2:
                        pool.wait_ge(h_step.sem, h_step.now(b, 2 * (n - 2) + 1))
                    nc.gpsimd.tensor_scalar(en1[:, n % 2], en[:, n % 2], 1.0, None, ALU.add).then_inc(en1_ready.sem, 1)

        @block.tensor
        def _(pe):
            pe.wait_ge(w_in, 48)
            pe.wait_ge(consts, 1)

            def turn(job, src, b):
                ring.wait_free(pe, job, b)
                for t in range(NT):
                    last = pe.transpose(p_r[ring.at(job)][0:src.shape[2], t * P:(t + 1) * P], src[:, t, :], ident[:])
                last.then_inc(ring.filled(job), 1)

            def sums(kind, g, k, first, last_k, b):
                job = (kind, g, k)
                V = Vs if kind == "s" else Vx
                rows = LAST if kind == "x" and k == NC - 1 else P
                pr.wait_filled(pe, job, b)
                lo, width = (0, T) if kind == "x" or k == 0 else (P, T - P)
                for j in range(HG):
                    at = j * width
                    mm = pe.matmul(p_pv[32 * j:32 * j + 32, lo:lo + width], V[0:rows, k, HG * g + j, :],
                                   probs[0:rows, pr.at(job), at:at + width], start=first, stop=last_k,
                                   skip_group_check=True)
                return mm

            def to_channels(kind, b):
                for t in range(NT):
                    job = (kind + "y", t)
                    ring.wait_free(pe, job, b)
                    if t == 0:
                        pe.wait_ge(sums_kept.sem, sums_kept.now(b, G if kind == "s" else 2 * G))
                    for g in range(G):
                        mm = pe.transpose(p_r[ring.at(job)][:, g * P:(g + 1) * P], yT[:, g, t * P:(t + 1) * P], ident[:])
                    mm.then_inc(ring.filled(job), 1)
                for t in range(NT):
                    ring.wait_emptied(pe, (kind + "y", t), b)
                turn(kind + "ycT", yrow, b)
                ring.wait_emptied(pe, kind + "ycT", b)
                job = kind + "proj"
                ring.wait_free(pe, job, b)
                w0 = W_PROJ if kind == "s" else W_XO
                for t in range(NT):
                    mm = pe.matmul(p_r[ring.at(job)][:, t * C:(t + 1) * C], ycT[:, t * P:(t + 1) * P], w[:, w0:w0 + C],
                                   start=True, stop=True)
                mm.then_inc(ring.filled(job), 1)

            for b in range(B):
                pe.wait_ge(xn_ready.sem, xn_ready.now(b, 2))
                turn("xn1T", xn, b)
                ring.wait_emptied(pe, "xn1T", b)
                ring.wait_free(pe, "qk", b)
                for i in range(2):
                    mm = pe.matmul(p_r[ring.at("qk")][:, i * T:(i + 1) * T], w[:, W_QKV + i * C:W_QKV + (i + 1) * C],
                                   xnT[:], start=True, stop=True)
                mm.then_inc(ring.filled("qk"), 1)
                ring.wait_free(pe, "v", b)
                for t in range(NT):
                    mm = pe.matmul(p_r[ring.at("v")][:, t * C:(t + 1) * C], xnT[:, t * P:(t + 1) * P],
                                   w[:, W_QKV + 2 * C:W_QKV + 3 * C], start=True, stop=True)
                mm.then_inc(ring.filled("v"), 1)
                pe.wait_ge(ctx_in.sem, ctx_in.now(b))
                for n, (k0, width) in enumerate(KBANKS):
                    ring.wait_free(pe, ("k", n), b)
                    pe.matmul(p_r[ring.at(("k", n))][:, 0:width], w[:, W_XK:W_XK + C], ctx_sb[:, k0:k0 + width],
                              start=True, stop=True).then_inc(ring.filled(("k", n)), 1)
                for n, chunks in enumerate(VGROUPS):
                    ring.wait_free(pe, ("vx", n), b)
                    for i, c in enumerate(chunks):
                        rows = min(P, S - c * P)
                        mm = pe.matmul(p_r[ring.at(("vx", n))][0:rows, i * C:(i + 1) * C], ctx_sb[:, c * P:c * P + rows],
                                       w[:, W_XV:W_XV + C], start=True, stop=True)
                    mm.then_inc(ring.filled(("vx", n)), 1)
                pe.wait_ge(sqk_packed.sem, sqk_packed.now(b))
                ring.wait_free(pe, "score0", b)
                for t in range(NT):
                    mm = pe.matmul(p_r[ring.at("score0")][:, t * T:(t + 1) * T], Qs[0:QK_ROWS, 0, 0, t * P:(t + 1) * P],
                                   Ks[0:QK_ROWS, 0, :], start=True, stop=True)
                mm.then_inc(ring.filled("score0"), 1)
                ring.wait_emptied(pe, "score0", b)
                ring.wait_free(pe, "ff", b)
                o = p_r[ring.at("ff")]
                pe.matmul(o[:, 0:T], neg_before[:], S0[:, 0, :], start=True, stop=True)
                pe.matmul(o[:, T:2 * T], neg_ones[:], S0[:, 0, :], start=True, stop=False)
                pe.matmul(o[:, T:2 * T], neg_before[:], S0[:, 1, :], start=False,
                          stop=True).then_inc(ring.filled("ff"), 1)
                pe.wait_ge(bias_ready.sem, bias_ready.now(b))
                ring.wait_free(pe, "biasT", b)
                o = p_r[ring.at("biasT")]
                pe.transpose(o[:, 0:P], bias[:, 0, 0:P], ident[:])
                pe.transpose(o[:, P:2 * P], bias[:, 1, 0:P], ident[:])
                pe.transpose(o[:, 2 * P:3 * P], bias[:, 1, P:T], ident[:]).then_inc(ring.filled("biasT"), 1)
                for h in range(H):
                    job = ("smax", h)
                    ring.wait_free(pe, job, b)
                    o = p_r[ring.at(job)]
                    q, k = Qs[0:QK_ROWS, h // 2, h % 2], Ks[0:QK_ROWS, h // 2]
                    pe.matmul(o[:, 0:P], q[:, 0:P], k[:, 0:P], start=True, stop=True)
                    pe.matmul(o[:, P:P + T], q[:, P:T], k, start=True,
                              stop=True).then_inc(ring.filled(job), 1)
                ring.wait_emptied(pe, ("smax", H - 1), b)
                turn("smT", smax, b)
                pe.wait_ge(sm_packed.sem, sm_packed.now(b))
                for i in range(G * NT + 1):
                    if i < G * NT:
                        g, k = divmod(i, NT)
                        job = ("s", g, k)
                        wait_scores_taken(pe, job, b)
                        lo, width = (0, T) if k == 0 else (P, T - P)
                        for j in range(2):
                            mm = pe.matmul(p_sc[sc.at(job)][:, j, 0:2 * width], Ks[0:ALL_ROWS, 2 * g + j, k * P:(k + 1) * P],
                                           Qs[0:ALL_ROWS, 2 * g + j, :, lo:lo + width], start=True, stop=True)
                        mm.then_inc(sc.filled(job), 1)
                    if i > 0:
                        g, k = divmod(i - 1, NT)
                        if k == 0:
                            wait_past(pe, sums_kept.sem, sums_kept.now(b, g))
                        mm = sums("s", g, k, k == 0, k == NT - 1, b)
                        mm.then_inc(pr.emptied(("s", g, k)), 1)
                to_channels("s", b)
                pe.wait_ge(xn_ready.sem, xn_ready.now(b, 4))
                turn("xn2T", xn, b)
                ring.wait_emptied(pe, "xn2T", b)
                ring.wait_free(pe, "q2", b)
                pe.matmul(p_r[ring.at("q2")][:, 0:T], w[:, W_XQ:W_XQ + C], xnT[:], start=True,
                          stop=True).then_inc(ring.filled("q2"), 1)
                pe.wait_ge(q2_packed.sem, q2_packed.now(b))
                pe.wait_ge(xk_packed.sem, xk_packed.now(b))
                for step in cross:
                    if step[0] == "xmax":
                        _, g, t, j, n = step
                        h = HG * g + j
                        k0, width = PIECES[n]
                        ring.wait_free(pe, step, b)
                        pe.matmul(p_r[ring.at(step)][:, 0:width], Qx[0:QK_ROWS, h // 2, h % 2, t * P:(t + 1) * P],
                                  Kx[0:QK_ROWS, h // 2, k0:k0 + width], start=True, stop=True).then_inc(ring.filled(step), 1)
                    elif step[0] == "xmT":
                        g = step[1]
                        pe.wait_ge(xmax_ready.sem, xmax_ready.now(b, g + 1))
                        turn(step, xmax[:, g % 2], b)
                    elif step[0] == "score":
                        _, g, c = step
                        job = ("x", g, c)
                        rows = min(P, S - c * P)
                        if c == 0:
                            pe.wait_ge(xm_packed.sem, xm_packed.now(b, 32 * (g + 1)))
                        wait_scores_taken(pe, job, b)
                        for j in range(2):
                            mm = pe.matmul(p_sc[sc.at(job)][0:rows, j, :], Kx[0:ALL_ROWS, 2 * g + j, c * P:c * P + rows],
                                           Qx[0:ALL_ROWS, 2 * g + j, :, :], start=True, stop=True)
                        mm.then_inc(sc.filled(job), 1)
                    elif step[0] == "sum":
                        _, g, c = step
                        if c == 0:
                            pe.wait_ge(sums_kept.sem, sums_kept.now(b, G + g))
                        mm = sums("x", g, c, c == 0, c == NC - 1, b)
                        mm.then_inc(pr.emptied(("x", g, c)), 1)
                to_channels("x", b)
                pe.wait_ge(xn_ready.sem, xn_ready.now(b, 6))
                turn("xn3T", xn, b)
                ring.wait_emptied(pe, "xn3T", b)
                ring.wait_free(pe, "router", b)
                for t in range(NT):
                    mm = pe.matmul(p_r[ring.at("router")][:, t * E_RT:(t + 1) * E_RT], xnT[:, t * P:(t + 1) * P],
                                   w[:, W_R:W_R + E_RT], start=True, stop=True)
                mm.then_inc(ring.filled("router"), 1)
                pe.wait_ge(gates_ready.sem, gates_ready.now(b))
                turn("gatesT", gates, b)
                for n in range(NB):
                    job = ("h13", n)
                    ring.wait_free(pe, job, b)
                    for i, w0 in enumerate((W_1, W_3)):
                        mm = pe.matmul(p_r[ring.at(job)][:, i * T:(i + 1) * T], w[:, w0 + n * P:w0 + (n + 1) * P], xnT[:],
                                       start=True, stop=True)
                    mm.then_inc(ring.filled(job), 1)
                    if n < NB_RT:
                        job = ("gate", n)
                        if n == 0:
                            ring.wait_emptied(pe, "gatesT", b)
                        ring.wait_free(pe, job, b)
                        pe.matmul(p_r[ring.at(job)][:, 0:T], expert_rows[:, n, :], gatesT[:], start=True,
                                  stop=True).then_inc(ring.filled(job), 1)
                for n in range(NB):
                    ring.wait_emptied(pe, ("gate", n) if n < NB_RT else ("h13", n), b)
                ring.wait_free(pe, "ffn", b)
                for t in range(NT):
                    for n in range(NB):
                        mm = pe.matmul(p_r[ring.at("ffn")][:, t * C:(t + 1) * C], hT[:, n, t * P:(t + 1) * P],
                                       w[:, W_2 + n * P:W_2 + (n + 1) * P], start=(n == 0), stop=(n == NB - 1))
                mm.then_inc(ring.filled("ffn"), 1)

        @block.scalar
        def _(act):
            act.wait_ge(w_in, 48)
            act.wait_ge(colbs_ready, 1)

            def evacuate(dst, job, width, b, parts=P, **kw):
                ring.wait_filled(act, job, b)
                nc.scalar.activation(dst, p_r[ring.at(job)][0:parts, 0:width], kw.pop("func", ACT.Copy), **kw).then_inc(
                    ring.emptied(job), 1)

            def keep_sums(kind, g, b):
                pr.wait_emptied(act, (kind, g, NT - 1 if kind == "s" else NC - 1), b)
                nc.scalar.activation(yT[:, g, :], p_pv[:, 0:T], ACT.Copy).then_inc(sums_kept.sem, 1)

            for b in range(B):
                evacuate(xnT[:], "xn1T", T, b)
                ring.wait_filled(act, "qk", b)
                nc.scalar.activation(qk[:, 0, :], p_r[ring.at("qk")][:, 0:T], ACT.Identity, bias=colbs[:, B_Q:B_Q + 1],
                                     scale=SCALE)
                nc.scalar.activation(qk[:, 1, :], p_r[ring.at("qk")][:, T:2 * T], ACT.Identity,
                                     bias=colb[:, B_K:B_K + 1]).then_inc(ring.emptied("qk"), 1)
                wait_past(act, kpart_ready.sem, kpart_ready.last(b))
                for n, (k0, width) in enumerate(KBANKS):
                    evacuate(kf[:, k0:k0 + width], ("k", n), width, b, func=ACT.Identity, bias=colb[:, B_XK:B_XK + 1])
                evacuate(biasT[:], "biasT", 3 * P, b)
                evacuate(sm_neg[:], "smT", T, b, parts=H, scale=-1.0)
                for i in range(G * NT):
                    g, k = divmod(i, NT)
                    job = ("s", g, k)
                    width = T if k == 0 else T - P
                    sc.wait_emptied(act, job, b)
                    pr.wait_free(act, job, b)
                    nc.scalar.activation(probs[:, pr.at(job), 0:HG * width], biased[:, i % 2, 0:HG * width],
                                         ACT.Exp).then_inc(pr.filled(job), 1)
                    if i >= 3 and i % 2 == 1:
                        keep_sums("s", (i - 3) // 2, b)
                keep_sums("s", G - 1, b)
                evacuate(ycT[:], "sycT", T, b)
                evacuate(xnT[:], "xn2T", T, b)
                evacuate(qk[:, 0, :], "q2", T, b, func=ACT.Identity, bias=colbs[:, B_XQ:B_XQ + 1], scale=SCALE)
                for step in cross:
                    if step[0] == "xmT":
                        g = step[1]
                        if g:
                            act.wait_ge(xm_ready.sem, xm_ready.now(b, g))
                        evacuate(xm_neg[:], step, T, b, parts=HG, scale=-1.0)
                    elif step[0] == "score":
                        _, g, c = step
                        job = ("x", g, c)
                        rows = min(P, S - c * P)
                        sc.wait_filled(act, job, b)
                        pr.wait_free(act, job, b)
                        nc.scalar.activation(probs[0:rows, pr.at(job), :], p_sc[sc.at(job)][0:rows].rearrange("p s n -> p (s n)"),
                                             ACT.Exp).then_inc(pr.filled(job), 1)
                    elif step[0] == "sum" and step[2] == 0 and step[1] > 0:
                        keep_sums("x", step[1] - 1, b)
                keep_sums("x", G - 1, b)
                evacuate(ycT[:], "xycT", T, b)
                evacuate(xnT[:], "xn3T", T, b)
                for t in range(NT):
                    act.wait_ge(gate_step.sem, gate_step.now(b, 5))
                    nc.scalar.activation(eg[:, t, :], logits[:, t, 0:E_RT], ACT.Exp,
                                         bias=neg_best[:, t, :]).then_inc(eg_ready.sem, 1)
                evacuate(gatesT[:], "gatesT", T, b, parts=E_RT)
                for n in range(NB):
                    ring.wait_filled(act, ("h13", n), b)
                    if n >= 2:
                        act.wait_ge(en1_ready.sem, en1_ready.now(b, n - 1))
                    nc.scalar.activation(en[:, n % 2, :], p_r[ring.at(("h13", n))][:, 0:T], ACT.Exp,
                                         scale=-1.0).then_inc(en_ready.sem, 1)

        @block.vector
        def _(dve):
            for q in (Qs, Qx):
                nc.vector.memset(q[:].bitcast(F32), 0.0).then_inc(rows_set, 1)
            nc.vector.memset(Ks[QK_ROWS:P], 1.0).then_inc(rows_set, 1)
            dve.wait_ge(w_in, 48)
            nc.vector.tensor_scalar(colbs[:], colb[:, 0:2], SCALE, None, ALU.mult).then_inc(colbs_ready, 1)
            dve.wait_ge(consts, 1)

            def layer_norm(k, src, b):
                at = 4 * k
                for t in range(NT):
                    nc.vector.bn_stats(stats[:, t, :], src[:, t, :]).then_inc(ln_step.sem, 1)
                dve.wait_ge(ln_step.sem, ln_step.now(b, at + 2))
                for t in range(NT):
                    nc.vector.bn_aggr(mv[:, t, :], stats[:, t, :]).then_inc(ln_step.sem, 1)
                dve.wait_ge(ln_step.sem, ln_step.now(b, at + 4))
                dve.wait_ge(rstd_ready.sem, rstd_ready.now(b, k + 1))
                for t in range(NT):
                    nc.vector.tensor_scalar(xn[:, t, :], src[:, t, :], mv[:, t, 0:1], rstd[:, t, :], ALU.subtract,
                                            ALU.mult).then_inc(xn_ready.sem, 1)

            def split(k, n, b):
                nc.vector.tensor_copy(qk_part[:, 0, 0:n, :], qk[:, 0:n, :]).then_inc(part_step.sem, 1)
                dve.wait_ge(part_step.sem, part_step.now(b, 3 * k + 1))
                nc.vector.tensor_tensor(qk_rest[:, 0:n, :], qk[:, 0:n, :], qk_part[:, 0, 0:n, :],
                                        ALU.subtract).then_inc(part_step.sem, 1)
                dve.wait_ge(part_step.sem, part_step.now(b, 3 * k + 2))
                nc.vector.tensor_copy(qk_part[:, 1, 0:n, :], qk_rest[:, 0:n, :]).then_inc(part_step.sem, 1)
                dve.wait_ge(part_step.sem, part_step.now(b, 3 * k + 3))
                nc.vector.tensor_tensor(qk_part[:, 2, 0:n, :], qk_rest[:, 0:n, :], qk_part[:, 1, 0:n, :],
                                        ALU.subtract).then_inc(part_ready.sem, 1)

            def normalise(kind, k, b):
                for t in range(NT):
                    job = (kind + "y", t)
                    ring.wait_filled(dve, job, b)
                    v = p_r[ring.at(job)][:].rearrange("p (h c) -> p h c", c=32)
                    nc.vector.reciprocal(rden[:, t, :], v[:, :, D]).then_inc(rden_ready.sem, 1)
                    dve.wait_ge(rden_ready.sem, rden_ready.now(b, 2 * k + t + 1))
                    nc.vector.tensor_tensor(yrow[:, t, :].rearrange("p (h d) -> p h d", d=D), v[:, :, 0:D],
                                            rden[:, t, :].unsqueeze(2).to_broadcast([P, H, D]),
                                            ALU.mult).then_inc(ring.emptied(job), 1)

            for b in range(B):
                dve.wait_ge(x_in.sem, x_in.now(b))
                layer_norm(0, xin, b)
                ring.wait_emptied(dve, "qk", b)
                split(0, 2, b)
                if b == 0:
                    nc.vector.memset(Kx[QK_ROWS:P], 1.0).then_inc(rows_set, 1)
                ring.wait_filled(dve, "v", b)
                nc.vector.tensor_tensor(Vs[:, :, :, 0:D], p_r[ring.at("v")][:, 0:NT * C].rearrange("p (t h d) -> p t h d", t=NT, d=D),
                                        rowb[:, R_V:R_V + C].rearrange("p (h d) -> p h d", d=D).unsqueeze(1).to_broadcast([P, NT, H, D]),
                                        ALU.add).then_inc(ring.emptied("v"), 1)
                for n, chunks in enumerate(VGROUPS):
                    ring.wait_filled(dve, ("vx", n), b)
                    m, rows = len(chunks), min(P, S - chunks[-1] * P)
                    nc.vector.tensor_tensor(Vx[0:rows, chunks[0]:chunks[-1] + 1, :, 0:D],
                                            p_r[ring.at(("vx", n))][0:rows, 0:m * C].rearrange("p (t h d) -> p t h d", t=m, d=D),
                                            rowb[0:rows, R_XV:R_XV + C].rearrange("p (h d) -> p h d", d=D).unsqueeze(1).to_broadcast([rows, m, H, D]),
                                            ALU.add).then_inc(ring.emptied(("vx", n)), 1)
                ring.wait_filled(dve, "score0", b)
                nc.vector.scalar_tensor_tensor(out=S0[:], in0=p_r[ring.at("score0")][:].rearrange("p (t n) -> p t n", t=NT),
                                               scalar=0.0, in1=earlier[:], op0=ALU.max,
                                               op1=ALU.mult).then_inc(ring.emptied("score0"), 1)
                ring.wait_filled(dve, "ff", b)
                nc.vector.tensor_tensor(nff[:, :, 0:T], p_r[ring.at("ff")][:].rearrange("p (t n) -> p t n", t=NT), acausal[:],
                                        ALU.add).then_inc(ring.emptied("ff"), 1)
                ring.wait_emptied(dve, "ff", b)
                for r in range(ROUNDS):
                    for t in range(NT):
                        src = nff[:, t, :] if r == 0 else top[:, (r - 1) % 2, t, :]
                        if r:
                            dve.wait_ge(top_step.sem, top_step.now(b, 4 * r - 1 + t))
                        nc.vector.max(top8[:, t, :], src).then_inc(top_step.sem, 1)
                    for t in range(NT):
                        src = nff[:, t, :] if r == 0 else top[:, (r - 1) % 2, t, :]
                        dve.wait_ge(top_step.sem, top_step.now(b, 4 * r + t + 1))
                        nc.vector.match_replace(top[:, r % 2, t, :], top8[:, t, :], src, TAKEN).then_inc(top_step.sem, 1)
                dve.wait_ge(top_step.sem, top_step.now(b))
                nc.vector.scalar_tensor_tensor(out=drop[:], in0=top[:, (ROUNDS - 1) % 2, :, 0:T], scalar=TAKEN_BELOW,
                                               in1=off_diag[:], op0=ALU.is_gt, op1=ALU.mult).then_inc(drop_ready.sem, 1)
                dve.wait_ge(drop_ready.sem, drop_ready.now(b))
                nc.vector.tensor_tensor(bias[:], drop[:], nff[:, :, 0:T], ALU.add).then_inc(bias_ready.sem, 1)
                dve.wait_ge(bias_ready.sem, bias_ready.now(b))
                for h in range(H):
                    job = ("smax", h)
                    ring.wait_filled(dve, job, b)
                    if h >= 2:
                        ring.wait_emptied(dve, ("smax", h - 2), b)
                    o = p_r[ring.at(job)]
                    nc.vector.tensor_tensor_reduce(junk[:, h % 2, 0, 0:P], o[:, 0:P], bias[:, 0, 0:P], 1.0, TAKEN, ALU.add,
                                                   ALU.max, smax[:, 0, h:h + 1]).then_inc(smax_first.sem, 1)
                    nc.vector.tensor_tensor_reduce(junk[:, h % 2, 1, :], o[:, P:P + T], bias[:, 1, :], 1.0, TAKEN, ALU.add,
                                                   ALU.max, smax[:, 1, h:h + 1]).then_inc(ring.emptied(job), 1)
                for i in range(G * NT):
                    g, k = divmod(i, NT)
                    job = ("s", g, k)
                    width = T if k == 0 else T - P
                    sc.wait_filled(dve, job, b)
                    if i == 0:
                        ring.wait_emptied(dve, "biasT", b)
                    if i >= 2:
                        pr.wait_filled(dve, exp_jobs[i - 2], b)
                    four = [P, 2, 2, width]
                    nc.vector.tensor_tensor(biased[:, i % 2, 0:HG * width].rearrange("p (s q n) -> p s q n", s=2, q=2),
                                            p_sc[sc.at(job)][:, :, 0:2 * width].rearrange("p s (q n) -> p s q n", q=2),
                                            biasT[:, k * T:k * T + width].unsqueeze(1).unsqueeze(1).to_broadcast(four),
                                            ALU.add).then_inc(sc.emptied(job), 1)
                normalise("s", 0, b)
                ring.wait_filled(dve, "sproj", b)
                dve.wait_ge(xb_ready.sem, xb_ready.now(b))
                nc.vector.tensor_tensor(x1[:], p_r[ring.at("sproj")][:, 0:NT * C].rearrange("p (t c) -> p t c", t=NT), xb[:],
                                        ALU.add).then_inc(ring.emptied("sproj"), 1)
                ring.wait_emptied(dve, "sproj", b)
                layer_norm(1, x1, b)
                ring.wait_emptied(dve, "q2", b)
                split(1, 1, b)
                for step in cross:
                    if step[0] == "xmax":
                        _, g, t, j, n = step
                        ring.wait_filled(dve, step, b)
                        nc.vector.tensor_reduce(xmax4[:, g % 2, t, j, n:n + 1], p_r[ring.at(step)][:, 0:PIECES[n][1]], AX.X,
                                                ALU.max).then_inc(ring.emptied(step), 1)
                    elif step[0] == "xmax8":
                        g = step[1]
                        ring.wait_emptied(dve, ("xmax", g, NT - 1, HG - 1, 3), b)
                        nc.vector.tensor_reduce(xmax[:, g % 2], xmax4[:, g % 2], AX.X, ALU.max).then_inc(xmax_ready.sem, 1)
                normalise("x", 1, b)
                ring.wait_filled(dve, "xproj", b)
                dve.wait_ge(x1b_ready.sem, x1b_ready.now(b))
                nc.vector.tensor_tensor(x2[:], p_r[ring.at("xproj")][:, 0:NT * C].rearrange("p (t c) -> p t c", t=NT), x1b[:],
                                        ALU.add).then_inc(ring.emptied("xproj"), 1)
                ring.wait_emptied(dve, "xproj", b)
                layer_norm(2, x2, b)
                ring.wait_filled(dve, "router", b)
                nc.vector.tensor_tensor(logits[:, :, 0:E_RT], p_r[ring.at("router")][:, 0:NT * E_RT].rearrange("p (t e) -> p t e", t=NT),
                                        rowb[:, R_R:R_R + E_RT].unsqueeze(1).to_broadcast([P, NT, E_RT]),
                                        ALU.add).then_inc(ring.emptied("router"), 1)
                ring.wait_emptied(dve, "router", b)
                for t in range(NT):
                    nc.vector.max(best8[:, t, :], logits[:, t, :]).then_inc(gate_step.sem, 1)
                dve.wait_ge(gate_step.sem, gate_step.now(b, 2))
                for t in range(NT):
                    nc.vector.match_replace(ranked[:, t, :], best8[:, t, :], logits[:, t, :], TAKEN).then_inc(gate_step.sem, 1)
                nc.vector.tensor_scalar(neg_best[:], best8[:, :, GDUMMY:GDUMMY + 1], -1.0, None,
                                        ALU.mult).then_inc(gate_step.sem, 1)
                dve.wait_ge(eg_ready.sem, eg_ready.now(b))
                dve.wait_ge(gate_step.sem, gate_step.now(b, 5))
                nc.vector.scalar_tensor_tensor(out=egm[:], in0=ranked[:, :, 0:E_RT], scalar=TAKEN_BELOW, in1=eg[:],
                                               op0=ALU.is_lt, op1=ALU.mult).then_inc(gate_step.sem, 1)
                dve.wait_ge(gate_step.sem, gate_step.now(b, 6))
                nc.vector.tensor_reduce(gsum[:], egm[:], AX.X, ALU.add).then_inc(gate_step.sem, 1)
                dve.wait_ge(gate_step.sem, gate_step.now(b, 7))
                nc.vector.reciprocal(grec[:], gsum[:]).then_inc(gate_step.sem, 1)
                dve.wait_ge(gate_step.sem, gate_step.now(b, 8))
                nc.vector.tensor_tensor(gates[:], egm[:], grec[:].to_broadcast([P, NT, E_RT]),
                                        ALU.mult).then_inc(gates_ready.sem, 1)
                for n in range(NB):
                    k = n % 2
                    dve.wait_ge(en1_ready.sem, en1_ready.now(b, n + 1))
                    nc.vector.reciprocal(sg[:, k, :], en1[:, k, :]).then_inc(h_step.sem, 1)
                    dve.wait_ge(h_step.sem, h_step.now(b, 2 * n + 1))
                    ring.wait_filled(dve, ("h13", n), b)
                    o = p_r[ring.at(("h13", n))]
                    nc.vector.tensor_tensor(hs[:, k, :], o[:, 0:T], sg[:, k, :], ALU.mult).then_inc(h_step.sem, 1)
                    dve.wait_ge(h_step.sem, h_step.now(b, 2 * n + 2))
                    routed = n < NB_RT
                    if routed and n >= 2:
                        ring.wait_emptied(dve, ("gate", n - 2), b)
                    nc.vector.tensor_tensor(hu[:, k, :] if routed else hT[:, n, :], o[:, T:2 * T], hs[:, k, :],
                                            ALU.mult).then_inc(ring.emptied(("h13", n)), 1)
                    if routed:
                        ring.wait_filled(dve, ("gate", n), b)
                        ring.wait_emptied(dve, ("h13", n), b)
                        nc.vector.tensor_tensor(hT[:, n, :], p_r[ring.at(("gate", n))][:, 0:T], hu[:, k, :],
                                                ALU.mult).then_inc(ring.emptied(("gate", n)), 1)
                ring.wait_filled(dve, "ffn", b)
                wait_past(dve, stored.sem, stored.last(b))
                nc.vector.tensor_tensor(xout[:], p_r[ring.at("ffn")][:, 0:NT * C].rearrange("p (t c) -> p t c", t=NT), x2[:],
                                        ALU.add).then_inc(ring.emptied("ffn"), 1)


def kernel(x, ctx_1024, L0_attn_w_attn, L0_attn_b_attn, L0_attn_w_proj, L0_attn_b_proj, L0_xattn_Wq, L0_xattn_bq,
           L0_xattn_Wk, L0_xattn_bk, L0_xattn_Wv, L0_xattn_bv, L0_xattn_Wo, L0_xattn_bo, L0_ffn_router_w,
           L0_ffn_router_b, L0_ffn_routed_w1, L0_ffn_routed_w3, L0_ffn_routed_w2, L0_ffn_shared_w1,
           L0_ffn_shared_w3, L0_ffn_shared_w2):
    import concourse.bacc as bacc
    from concourse.bass_utils import run_bass_kernel_spmd

    def wide(routed, shared):
        both = np.concatenate([np.asarray(routed), np.asarray(shared)], 0)
        return both.transpose(1, 0, 2).reshape(C, -1)

    w2 = np.concatenate([np.asarray(L0_ffn_routed_w2), np.asarray(L0_ffn_shared_w2)], 0)
    w2 = w2.reshape(NB, P, C).transpose(1, 0, 2).reshape(P, NB * C)
    b_attn = np.asarray(L0_attn_b_attn)
    arrays = {
        "x": np.asarray(x),
        "ctxT": np.asarray(ctx_1024).transpose(0, 2, 1),
        "w_all": np.concatenate([np.asarray(L0_attn_w_attn).T, np.asarray(L0_attn_w_proj).T, np.asarray(L0_xattn_Wq).T,
                                 np.asarray(L0_xattn_Wk).T, np.asarray(L0_xattn_Wv).T, np.asarray(L0_xattn_Wo).T,
                                 np.asarray(L0_ffn_router_w), wide(L0_ffn_routed_w1, L0_ffn_shared_w1),
                                 wide(L0_ffn_routed_w3, L0_ffn_shared_w3), w2], 1),
        "col_bias": np.stack([b_attn[0:C], np.asarray(L0_xattn_bq), b_attn[C:2 * C], np.asarray(L0_xattn_bk)], 1),
        "row_bias": np.concatenate([b_attn[2 * C:], np.asarray(L0_attn_b_proj), np.asarray(L0_xattn_bv),
                                    np.asarray(L0_xattn_bo), np.asarray(L0_ffn_router_b)])[None],
    }
    nc = bacc.Bacc("TRN2", target_bir_lowering=False, num_devices=1)
    arrays = {f"in_{k}": np.ascontiguousarray(v) for k, v in arrays.items()}
    args = [nc.dram_tensor(k, v.shape, mybir.dt.from_np(v.dtype), kind="ExternalInput").ap() for k, v in arrays.items()]
    args.append(nc.dram_tensor("out_x", (B, T, C), F32, kind="ExternalOutput").ap())
    build(nc, *args)
    return run_bass_kernel_spmd(nc, [arrays], core_ids=[0]).results[0]["out_x"]
```

```python
from contextlib import ExitStack

import numpy as np

import concourse.bass as bass
from concourse import mybir

F32 = mybir.dt.float32
BF16 = mybir.dt.bfloat16
ALU = mybir.AluOpType
ACT = mybir.ActivationFunctionType
AX = mybir.AxisListType

B, T, C, S = 4, 256, 128, 1601
H = 16
D = C // H
P = 128
NT = T // P
NC = -(-S // P)
LAST = S - (NC - 1) * P
G = 4
HG = H // G
NP = H // 2
E_RT, E_SH, HID = 8, 2, 64
NB = (E_RT + E_SH) * HID // P
NB_RT = E_RT * HID // P
KEEP = 50
ROUNDS = 7
DUMMY = ROUNDS * 8 - KEEP
TOP = 2
GDUMMY = 8 - TOP
SCALE = float(1.0 / np.sqrt(np.float32(D)))
EPS = 1e-5
BIG = 1.0e30
TAKEN = -3.0e38
TAKEN_BELOW = -2.0e38

PARTS = 6
HEAD_ROWS = PARTS * D
QK_ROWS = 2 * HEAD_ROWS
VH = D + 1
VROW = H * VH
ALL_ROWS = QK_ROWS + 2

W_QKV, W_PROJ, W_XQ, W_XK, W_XV, W_XO = 0, 3 * C, 4 * C, 5 * C, 6 * C, 7 * C
W_R = 8 * C
W_1 = W_R + E_RT
W_3 = W_1 + NB * P
W_2 = W_3 + NB * P
W_ALL = W_2 + NB * P
B_Q, B_XQ, B_K, B_XK = range(4)
R_V, R_PROJ, R_XV, R_XO, R_R = 0, C, 2 * C, 3 * C, 4 * C
R_ALL = 4 * C + E_RT

PIECES = [(0, 401), (401, 400), (801, 400), (1201, 400)]
KBANKS = [(0, 512), (512, 512), (1024, 512), (1536, S - 1536)]
VGROUPS = [range(0, 4), range(4, 8), range(8, 12), range(12, 13)]



class Stage:

    def __init__(self, sem, per):
        self.sem, self.per = sem, per

    def now(self, b, n=None):
        return b * self.per + (self.per if n is None else n)

    def last(self, b, n=None):
        return (b - 1) * self.per + (self.per if n is None else n)


def wait_past(eng, sem, value):
    if value > 0:
        eng.wait_ge(sem, value)


class Slots:

    def __init__(self, filled, emptied, jobs, unsignalled=()):
        self.n = len(filled)
        self.jobs = jobs
        self.index = {job: i for i, job in enumerate(jobs)}
        self.filled_sems, self.emptied_sems = filled, emptied
        assert len(self.index) == len(jobs)
        self.fills, count = {}, [0] * self.n
        for i, (step, b) in enumerate(jobs):
            count[i % self.n] += step[0] not in unsignalled
            self.fills[step, b] = count[i % self.n]

    def at(self, job, b):
        return self.index[job, b] % self.n

    def use(self, job, b):
        return self.index[job, b] // self.n + 1

    def filled(self, job, b):
        return self.filled_sems[self.at(job, b)]

    def emptied(self, job, b):
        return self.emptied_sems[self.at(job, b)]

    def wait_filled(self, eng, job, b):
        eng.wait_ge(self.filled(job, b), self.fills[job, b])

    def wait_emptied(self, eng, job, b):
        eng.wait_ge(self.emptied(job, b), self.use(job, b))

    def wait_free(self, eng, job, b):
        wait_past(eng, self.emptied(job, b), self.use(job, b) - 1)


def build(nc, x, ctxT, w_all, col_bias, row_bias, out):
    with ExitStack() as ctx:
        def sb(name, shape, dt=F32):
            return ctx.enter_context(nc.sbuf_tensor(name, shape, dt))

        def ps(name, shape):
            return ctx.enter_context(nc.psum_tensor(name, shape, F32))

        def sem(name):
            return ctx.enter_context(nc.semaphore(name))

        w = sb("w", [P, W_ALL])
        colb = sb("colb", [P, 4])
        colbs = sb("colbs", [P, 2])
        rowb = sb("rowb", [P, R_ALL])
        ident = sb("ident", [P, P])
        neg_before = sb("neg_before", [P, P])
        neg_ones = sb("neg_ones", [P, P])
        earlier = sb("earlier", [P, NT, T])
        acausal = sb("acausal", [P, NT, T])
        off_diag = sb("off_diag", [P, NT, T])
        minus_half = sb("minus_half", [P, NT, 1])
        expert_rows = sb("expert_rows", [E_RT, NB_RT, P])
        xin = sb("xin", [P, NT, C])
        xb = sb("xb", [P, NT, C])
        ctx_sb = sb("ctx_sb", [P, S])
        stats = sb("stats", [P, 3, NT, 6])
        mv = sb("mv", [P, 3, NT, 2])
        rstd = sb("rstd", [P, 3, NT, 1])
        var_eps = sb("var_eps", [P, 3, NT, 1])
        xn = sb("xn", [P, 3, NT, C])
        xnT = sb("xnT", [P, 3, T])
        qk = [sb("qk", [P, 2, T]), sb("q2", [P, 1, T])]
        qk_part = [sb("qk_part", [P, 3, 2, T], BF16), sb("q2_part", [P, 3, 1, T], BF16)]
        Qs = sb("Qs", [P, NP, 2, T], BF16)
        Ks = sb("Ks", [P, NP, T], BF16)
        Vs = sb("Vs", [P, NT * VROW + 32 - VH])
        S0 = sb("S0", [P, NT, T])
        nff = sb("nff", [P, NT, T + DUMMY])
        top = sb("top", [P, 2, NT, T + DUMMY])
        top8 = sb("top8", [P, NT, 8])
        bias = sb("bias", [P, NT, T])
        biasT = sb("biasT", [P, 3 * P])
        junk = sb("junk", [P, 2, NT, T])
        ones = junk[:].bitcast(BF16).rearrange("p i t n -> p (i t n)")[0:2, 0:S]
        smax = sb("smax", [P, NT, H])
        sm_neg = sb("sm_neg", [H, T])
        sm_part = sb("sm_part", [H, 2, T], BF16)
        biased = sb("biased", [P, 2, HG * T])
        probs = sb("probs", [P, 4, HG * T])
        yT = {k: sb(k + "yT", [P, G, T]) for k in "sx"}
        rden = {k: sb(k + "rden", [P, NT, H]) for k in "sx"}
        yrow = {k: sb(k + "yrow", [P, NT, C]) for k in "sx"}
        ycT = {k: sb(k + "ycT", [P, T]) for k in "sx"}
        x1 = sb("x1", [P, NT, C])
        x1b = sb("x1b", [P, 2, NT, C])
        kf = sb("kf", [P, S])
        k_part = sb("k_part", [P, 3, S], BF16)
        Kx = sb("Kx", [P, NP, S], BF16)
        Qx = [sb(f"Qx{i}", [P, NP, 2, T], BF16) for i in range(2)]
        Vx = sb("Vx", [P, 2, NC * VROW + 32 - VH])
        xmax4 = sb("xmax4", [P, 2, NT, HG, 4])
        xmax = sb("xmax", [P, 2, NT, HG])
        xm_neg = sb("xm_neg", [HG, T])
        xm_part = sb("xm_part", [HG, 2, 2, T], BF16)
        x2 = sb("x2", [P, NT, C])
        logits = sb("logits", [P, NT, E_RT + GDUMMY])
        ranked = sb("ranked", [P, NT, E_RT + GDUMMY])
        best8 = sb("best8", [P, NT, 8])
        neg_best = sb("neg_best", [P, NT, 1])
        eg = sb("eg", [P, NT, E_RT])
        egm = sb("egm", [P, NT, E_RT])
        gates = sb("gates", [P, NT, E_RT])
        gsum = sb("gsum", [P, NT, 1])
        grec = sb("grec", [P, NT, 1])
        gatesT = sb("gatesT", [E_RT, T])
        en = sb("en", [P, 2, T])
        sg = sb("sg", [P, 2, T])
        h13 = sb("h13", [P, 2, 2, T])
        hT = sb("hT", [P, NB, T])
        xout = sb("xout", [P, NT, C])

        scr_q = nc.dram_tensor("scr_q", (H, D, 6, T), BF16, kind="Internal").ap()
        scr_q2 = nc.dram_tensor("scr_q2", (H, D, 6, T), BF16, kind="Internal").ap()
        scr_k = nc.dram_tensor("scr_k", (H, D, 6, T), BF16, kind="Internal").ap()
        scr_xk = [nc.dram_tensor(f"scr_xk{b}", (H, D, 6, S), BF16, kind="Internal").ap() for b in range(B)]

        p_sc = [ps(f"p_sc{i}", [P, 2, 512]) for i in range(2)]
        p_pv = ps("p_pv", [P, 512])
        p_r = [ps(f"p_r{i}", [P, 512]) for i in range(3)]

        N = G * NC
        prep = [(0, "load"), (1, ("stats", 0)), (2, ("norm", 0)), (3, "xn1T"), (5, "qk"), (15, "v"), (20, "xb")]
        prep += [(6 + i, ("split", 0, i)) for i in range(4)] + [(6 + n, ("k", n)) for n in range(4)]
        prep += [(10, "qk_write"), (12, "qk_read")] + [(10 + 3 * i, ("k_split", i)) for i in range(4)]
        prep += [(14, "score0"), (15, "ff")] + [(16 + r, ("top", r)) for r in range(ROUNDS)]
        prep += [(23, "drop"), (24, "bias"), (25, "biasT")]
        prep += [(26 + h // 2, ("smax", h)) for h in range(H)] + [(34, "smT"), (35, "sm_split"), (36, "sm_send")]
        prep += [(41 + 2 * g, ("ssum", g)) for g in range(G)]
        prep += [(38 + i, ("sscore", i)) for i in range(G * NT)] + [(39 + i, ("sexp", i)) for i in range(G * NT)]
        prep += [(22, "k_write")]
        prep += [(49 + t, ("sy", t)) for t in range(NT)] + [(51, "sycT"), (52, "sproj"), (53, ("stats", 1)),
                                                            (54, ("norm", 1)), (55, "xn2T"), (56, "q2")]
        prep += [(57 + i, ("split", 1, i)) for i in range(4)] + [(61, "q2_write"), (62, "q2_read")]
        tail = [(3 + t, ("xy", t)) for t in range(NT)] + [(5, "xycT"), (6, "xproj"), (7, ("stats", 2)),
                                                          (8, ("norm", 2)), (9, "xn3T"), (11, "router"), (12, "gate1"),
                                                          (13, "gate2"), (14, "gate3"), (15, "gatesT")]
        tail += [(16 + 2 * n, ("h13", n)) for n in range(NB)] + [(16 + 2 * n, ("en1", n)) for n in range(NB)]
        tail += [(18 + 2 * n, ("h", n)) for n in range(NB)] + [(21 + 2 * n, ("gate", n)) for n in range(NB_RT)]
        tail += [(28, "ffn"), (29, "store")]
        pieces = [("xmax", g, t, j, n) for g in range(G) for t in range(NT) for j in range(HG)
                  for n in range(len(PIECES))]
        PG = len(pieces) // G
        LEAD, TURN = PG + 12, 3
        FIRST = -(-LEAD * N // len(pieces)) + 64
        EARLY = 11
        events = []
        for b in range(B):
            t0 = N * b
            start = t0 - FIRST - (EARLY if b else 0)
            events += [(start + t, 1, step, b) for t, step in prep]
            events += [(start + (11 if b < 2 else 48) + n, 1, ("vx", n), b) for n in range(len(VGROUPS))]
            for g in range(G):
                t = t0 - N + NC * (g + 1) + 1 if b else start + 30
                events.append((t, 1, ("kx_read", g), b))
                events.append((t0 + NC * (g + 1) + 1, 1, ("keep", g), b))
            for i in range(N):
                g, c = divmod(i, NC)
                events.append((t0 + i, 1.2, ("score", g, c), b))
                events.append((t0 + i + 1, 3, ("sum", g, c), b))
            for m, piece in enumerate(pieces):
                at = lambda m: t0 + (m - LEAD) * N / len(pieces)
                events.append((int(at(m) // 1), 2, piece, b))
                if (m + 1) % PG == 0:
                    g = piece[1]
                    events.append((int(at(m) // 1), 2, ("xmax8", g), b))
                    events.append((int(at(m + TURN) // 1), 2.5, ("xmT", g), b))
            events += [(t0 + N + t, 1, step, b) for t, step in tail]
        events.sort(key=lambda e: (e[0], e[1]))
        order = [(step, b) for _, _, step, b in events]

        in_ring = {"xn1T", "xn2T", "xn3T", "qk", "v", "k", "vx", "score0", "ff", "biasT", "smax", "smT", "ssum", "sy",
                   "sycT", "sproj", "q2", "xmax", "xmT", "xy", "xycT", "xproj", "router", "gatesT", "h13", "gate", "ffn"}

        def kind(step):
            return step if isinstance(step, str) else step[0]

        ring_jobs = [(step, b) for step, b in order if kind(step) in in_ring]
        score_jobs = [(step, b) for step, b in order if kind(step) in ("sscore", "score")]
        exp_jobs = [(step, b) for step, b in order if kind(step) in ("sexp", "score")]

        stages = []

        def stage(name, per):
            stages.append(Stage(sem(name), per))
            return stages[-1]

        def slots(name, n, jobs, unsignalled=()):
            return Slots([sem(f"{name}_filled{i}") for i in range(n)], [sem(f"{name}_emptied{i}") for i in range(n)], jobs,
                         unsignalled)

        ring = slots("ring", 3, ring_jobs, unsignalled=("ssum",))
        sc = slots("scores", 2, score_jobs)
        pr = slots("probs", 4, exp_jobs)
        scores_added = stage("scores_added", G * NT)

        def wait_scores_taken(eng, job, b):
            i = sc.index[job, b] - sc.n
            if i >= 0:
                before, bb = score_jobs[i]
                if before[0] == "sscore":
                    eng.wait_ge(scores_added.sem, scores_added.now(bb, before[1] + 1))
                else:
                    pr.wait_filled(eng, before, bb)

        sums_kept = stage("sums_kept", G)
        w_in, rows_set, const_step, consts, colbs_ready, ones_set, ones_in = sem("w_in"), sem("rows_set"), sem("const_step"), sem("consts"), sem("colbs_ready"), sem("ones_set"), sem("ones_in")
        x_in, ctx_in = stage("x_in", 16), stage("ctx_in", 16)
        ln_step = [stage(f"ln{k}_step", 4) for k in range(3)]
        xn_ready = [stage(f"xn{k}_ready", 2) for k in range(3)]
        var_ready = [stage(f"var{k}_ready", 1) for k in range(3)]
        rstd_ready = [stage(f"rstd{k}_ready", 1) for k in range(3)]
        part_step = [stage("qk_part_step", 3), stage("q2_part_step", 3)]
        part_ready = [stage("qk_part_ready", 1), stage("q2_part_ready", 1)]
        sqk_written, sqk_packed = stage("sqk_written", 96), stage("sqk_packed", 48)
        q2_written, q2_packed = stage("q2_written", 48), stage("q2_packed", 32)
        top_step = stage("top_step", 4 * ROUNDS)
        drop_ready, bias_ready = stage("drop_ready", 1), stage("bias_ready", 1)
        smax_first = stage("smax_first", H)
        sm_step, sm_ready, sm_packed = stage("sm_step", 1), stage("sm_ready", 1), stage("sm_packed", 32)
        rden_ready = {k: stage(k + "rden_ready", NT) for k in "sx"}
        xb_ready, x1b_ready = stage("xb_ready", 1), stage("x1b_ready", 1)
        kpart_step, kpart_ready = stage("kpart_step", 3), stage("kpart_ready", 1)
        xk_written = stage("xk_written", 48)
        xk_packed = [stage(f"xk_packed{g}", 16) for g in range(G)]
        xmax_ready = stage("xmax_ready", G)
        xm_step, xm_ready = stage("xm_step", G), stage("xm_ready", G)
        xm_packed = [stage(f"xm_packed{g}", 32) for g in range(G)]
        gate_step, eg_ready, gates_ready = stage("gate_step", 8), stage("eg_ready", 2), stage("gates_ready", 1)
        en_ready, en1_ready = stage("en_ready", NB), stage("en1_ready", NB)
        rec_ready, h_step, h_ready = stage("rec_ready", NB), stage("h_step", NB), stage("h_ready", NB)
        stored = stage("stored", 16)

        block = ctx.enter_context(nc.Block())

        @block.sync
        def _(sp):
            sp.dma_start(w[:], w_all).then_inc(w_in, 16)
            sp.dma_start(colb[:], col_bias).then_inc(w_in, 16)
            sp.dma_start(rowb[:], row_bias.to_broadcast([P, R_ALL])).then_inc(w_in, 16)
            sp.wait_ge(ones_set, 1)
            for keys, n in ((Ks, T), (Kx, S)):
                sp.dma_start(keys[QK_ROWS:ALL_ROWS], ones[0:2, 0:n].unsqueeze(1).to_broadcast([2, NP, n])).then_inc(ones_in, 16)
            sp.wait_ge(rows_set, 1)

            def to_scratch(scratch, src, repeat, done):
                dst = scratch.rearrange("h d c n -> (h d) c n")
                n = src.shape[-1]
                for k, (c0, width) in enumerate(((0, 3), (3, 2), (5, 1))):
                    part = src[:, k:k + 1, :].to_broadcast([P, width, n]) if repeat else src[:, 0:width, :]
                    sp.dma_start(dst[:, c0:c0 + width, :], part).then_inc(done.sem, 16)

            def keys_from_scratch(dst, scratch, p0, p1, done):
                src = scratch.rearrange("(p s) d c n -> (s d c) p n", s=2)
                sp.dma_start(dst[0:QK_ROWS, p0:p1, :], src[:, p0:p1, :]).then_inc(done.sem, 16)

            def queries_from_scratch(dst, scratch, done):
                src = scratch.rearrange("(p s) d c n -> s (d c) p n", s=2)
                for s in range(2):
                    sp.dma_start(dst[s * HEAD_ROWS:(s + 1) * HEAD_ROWS, :, s, :], src[s]).then_inc(done.sem, 16)

            def max_rows(dst, part, p0, p1, done):
                for r in range(2):
                    row = dst[QK_ROWS + r:QK_ROWS + r + 1, p0:p1].rearrange("o p s n -> o (p s) n")
                    sp.dma_start(row, part[:, r, :]).then_inc(done.sem, 16)

            for step, b in order:
                if step == "load":
                    wait_past(sp, xn_ready[0].sem, xn_ready[0].last(b))
                    wait_past(sp, xb_ready.sem, xb_ready.last(b))
                    sp.dma_start(xin[:], x[b].rearrange("(t p) c -> p t c", p=P)).then_inc(x_in.sem, 16)
                    if b:
                        ring.wait_filled(sp, ("vx", 3), b - 1)
                    sp.dma_start(ctx_sb[:], ctxT[b]).then_inc(ctx_in.sem, 16)
                elif step == "qk_write":
                    sp.wait_ge(part_ready[0].sem, part_ready[0].now(b))
                    to_scratch(scr_q, qk_part[0][:, :, 0, :], True, sqk_written)
                    to_scratch(scr_k, qk_part[0][:, :, 1, :], False, sqk_written)
                elif step == "qk_read":
                    sp.wait_ge(sqk_written.sem, sqk_written.now(b))
                    queries_from_scratch(Qs, scr_q, sqk_packed)
                    keys_from_scratch(Ks, scr_k, 0, NP, sqk_packed)
                elif step == "k_write":
                    sp.wait_ge(kpart_ready.sem, kpart_ready.now(b))
                    to_scratch(scr_xk[b], k_part[:], False, xk_written)
                elif step[0] == "kx_read":
                    g = step[1]
                    sp.wait_ge(xk_written.sem, xk_written.now(b))
                    if b:
                        sc.wait_filled(sp, ("score", g, NC - 1), b - 1)
                    keys_from_scratch(Kx, scr_xk[b], 2 * g, 2 * g + 2, xk_packed[g])
                elif step == "sm_send":
                    sp.wait_ge(sm_ready.sem, sm_ready.now(b))
                    max_rows(Qs, sm_part, 0, NP, sm_packed)
                elif step == "q2_write":
                    sp.wait_ge(part_ready[1].sem, part_ready[1].now(b))
                    to_scratch(scr_q2, qk_part[1][:, :, 0, :], True, q2_written)
                elif step == "q2_read":
                    sp.wait_ge(q2_written.sem, q2_written.now(b))
                    sp.wait_ge(rows_set, 3)
                    if b > 1:
                        sc.wait_filled(sp, ("score", G - 1, NC - 1), b - 2)
                    queries_from_scratch(Qx[b % 2], scr_q2, q2_packed)
                elif step[0] == "xmT":
                    g = step[1]
                    sp.wait_ge(xm_ready.sem, xm_ready.now(b, g + 1))
                    max_rows(Qx[b % 2], xm_part[:, g % 2], 2 * g, 2 * g + 2, xm_packed[g])
                elif step == "store":
                    ring.wait_emptied(sp, "ffn", b)
                    sp.dma_start(out[b].rearrange("(t p) c -> p t c", p=P), xout[:]).then_inc(stored.sem, 16)
            sp.wait_ge(stored.sem, stored.now(B - 1))

        @block.gpsimd
        def _(pool):
            count = [0]

            def step(ins):
                count[0] += 1
                ins.then_inc(const_step, 1)
                pool.wait_ge(const_step, count[0])

            nc.gpsimd.memset(ident[:], 0.0)
            nc.gpsimd.memset(neg_before[:], -1.0)
            nc.gpsimd.memset(neg_ones[:], -1.0)
            nc.gpsimd.memset(earlier[:], 1.0)
            nc.gpsimd.memset(acausal[:], 0.0)
            nc.gpsimd.memset(off_diag[:], -BIG)
            nc.gpsimd.memset(expert_rows[:], 1.0)
            nc.gpsimd.memset(Vs[:], 0.0)
            nc.gpsimd.memset(minus_half[:], -0.5)
            nc.gpsimd.memset(nff[:, :, T:], 1.0)
            nc.gpsimd.memset(logits[:, :, E_RT:], 3.0e38)
            step(nc.gpsimd.memset(Vx[:], 0.0))
            nc.gpsimd.memset(Vs[:, 0:NT * VROW].rearrange("p (h d) -> p h d", d=VH)[:, :, D:VH], 1.0)
            for i in range(2):
                nc.gpsimd.memset(Vx[:, i, 0:NC * VROW].rearrange("p (h d) -> p h d", d=VH)[:, :, D:VH], 1.0)
            nc.gpsimd.affine_select(out=ident[:], in_=ident[:], compare_op=ALU.not_equal, fill=1.0, base=0,
                                    pattern=[[-1, P]], channel_multiplier=1)
            nc.gpsimd.affine_select(out=neg_before[:], in_=neg_before[:], compare_op=ALU.is_gt, fill=0.0, base=0,
                                    pattern=[[1, P]], channel_multiplier=-1)
            nc.gpsimd.affine_select(out=acausal[:], in_=acausal[:], compare_op=ALU.is_ge, fill=-BIG, base=0,
                                    pattern=[[P, NT], [-1, T]], channel_multiplier=1)
            nc.gpsimd.affine_select(out=off_diag[:], in_=off_diag[:], compare_op=ALU.not_equal, fill=0.0, base=0,
                                    pattern=[[P, NT], [-1, T]], channel_multiplier=1)
            step(nc.gpsimd.affine_select(out=earlier[:], in_=earlier[:], compare_op=ALU.is_gt, fill=0.0, base=0,
                                         pattern=[[P, NT], [-1, T]], channel_multiplier=1))
            nc.gpsimd.memset(earlier[:, :, 0:1], 0.0)
            step(nc.gpsimd.affine_select(out=expert_rows[:], in_=expert_rows[:], compare_op=ALU.is_ge, fill=0.0,
                                         base=0, pattern=[[P, NB_RT], [1, P]], channel_multiplier=-HID))
            nc.gpsimd.affine_select(out=expert_rows[:], in_=expert_rows[:], compare_op=ALU.is_ge, fill=0.0,
                                    base=HID - 1, pattern=[[-P, NB_RT], [-1, P]],
                                    channel_multiplier=HID).then_inc(consts, 1)
            pool.wait_ge(w_in, 48)

            def row(r0):
                return rowb[:, r0:r0 + C].unsqueeze(1).to_broadcast([P, NT, C])

            for step, b in order:
                if step[0] == "stats":
                    k = step[1]
                    pool.wait_ge(ln_step[k].sem, ln_step[k].now(b))
                    nc.gpsimd.tensor_scalar(var_eps[:, k], mv[:, k, :, 1:2], EPS, None, ALU.add).then_inc(var_ready[k].sem, 1)
                    pool.wait_ge(var_ready[k].sem, var_ready[k].now(b))
                    nc.gpsimd.tensor_tensor(rstd[:, k], var_eps[:, k], minus_half[:], ALU.pow).then_inc(rstd_ready[k].sem, 1)
                elif step == "xb":
                    pool.wait_ge(x_in.sem, x_in.now(b))
                    if b:
                        ring.wait_emptied(pool, "sproj", b - 1)
                    nc.gpsimd.tensor_tensor(xb[:], xin[:], row(R_PROJ), ALU.add).then_inc(xb_ready.sem, 1)
                elif step[0] == "k_split":
                    i = step[1]
                    if i in (1, 3):
                        pool.wait_ge(kpart_step.sem, kpart_step.now(b, i))
                    if i == 1:
                        nc.gpsimd.tensor_tensor(kf[:], kf[:], k_part[:, 0, :], ALU.subtract).then_inc(kpart_step.sem, 1)
                    elif i == 3:
                        nc.gpsimd.tensor_tensor(k_part[:, 2, :], kf[:], k_part[:, 1, :],
                                                ALU.subtract).then_inc(kpart_ready.sem, 1)
                elif step == "sm_split":
                    ring.wait_emptied(pool, "smT", b)
                    nc.gpsimd.tensor_copy(sm_part[:, 0, :], sm_neg[:]).then_inc(sm_step.sem, 1)
                    pool.wait_ge(sm_step.sem, sm_step.now(b))
                    nc.gpsimd.tensor_tensor(sm_part[:, 1, :], sm_neg[:], sm_part[:, 0, :],
                                            ALU.subtract).then_inc(sm_ready.sem, 1)
                elif step == "q2":
                    ring.wait_emptied(pool, "sproj", b)
                    if b > 1:
                        ring.wait_emptied(pool, "xproj", b - 2)
                    nc.gpsimd.tensor_tensor(x1b[:, b % 2], x1[:], row(R_XO), ALU.add).then_inc(x1b_ready.sem, 1)
                elif step[0] == "xmT":
                    g = step[1]
                    ring.wait_emptied(pool, step, b)
                    if g >= 2:
                        pool.wait_ge(xm_packed[g - 2].sem, xm_packed[g - 2].now(b))
                    elif b:
                        pool.wait_ge(xm_packed[G - 2 + g].sem, xm_packed[G - 2 + g].last(b))
                    nc.gpsimd.tensor_copy(xm_part[:, g % 2, 0, :], xm_neg[:]).then_inc(xm_step.sem, 1)
                    pool.wait_ge(xm_step.sem, xm_step.now(b, g + 1))
                    nc.gpsimd.tensor_tensor(xm_part[:, g % 2, 1, :], xm_neg[:], xm_part[:, g % 2, 0, :],
                                            ALU.subtract).then_inc(xm_ready.sem, 1)
                elif step[0] == "en1":
                    n = step[1]
                    pool.wait_ge(en_ready.sem, en_ready.now(b, n + 1))
                    nc.gpsimd.tensor_scalar(en[:, n % 2], en[:, n % 2], 1.0, None, ALU.add).then_inc(en1_ready.sem, 1)
                elif step[0] == "h":
                    n = step[1]
                    k = n % 2
                    pool.wait_ge(rec_ready.sem, rec_ready.now(b, n + 1))
                    ring.wait_emptied(pool, ("h13", n), b)
                    nc.gpsimd.tensor_tensor(sg[:, k, :], h13[:, k, 0, :], sg[:, k, :], ALU.mult).then_inc(h_step.sem, 1)
                    pool.wait_ge(h_step.sem, h_step.now(b, n + 1))
                    nc.gpsimd.tensor_tensor(sg[:, k, :] if n < NB_RT else hT[:, n, :], h13[:, k, 1, :], sg[:, k, :],
                                            ALU.mult).then_inc(h_ready.sem, 1)

        @block.tensor
        def _(pe):
            pe.wait_ge(w_in, 48)
            pe.wait_ge(consts, 1)

            def turn(job, src, b):
                ring.wait_free(pe, job, b)
                for t in range(NT):
                    last = pe.transpose(p_r[ring.at(job, b)][0:src.shape[2], t * P:(t + 1) * P], src[:, t, :], ident[:])
                last.then_inc(ring.filled(job, b), 1)

            def sums(out_ps, V, probs_at, rows, g, k, lo, width, first, last_k):
                for j in range(HG):
                    v0 = k * VROW + (HG * g + j) * VH
                    mm = pe.matmul(out_ps[32 * j:32 * j + 32, lo:lo + width], V[0:rows, v0:v0 + 32],
                                   probs[0:rows, probs_at, j * width:(j + 1) * width], start=first, stop=last_k,
                                   skip_group_check=True)
                return mm

            for step, b in order:
                name = kind(step)
                o = p_r[ring.at(step, b)] if name in in_ring else None
                if name == "xn1T":
                    pe.wait_ge(xn_ready[0].sem, xn_ready[0].now(b))
                    turn(step, xn[:, 0], b)
                elif name == "qk":
                    ring.wait_emptied(pe, "xn1T", b)
                    ring.wait_free(pe, step, b)
                    for i in range(2):
                        mm = pe.matmul(o[:, i * T:(i + 1) * T], w[:, W_QKV + i * C:W_QKV + (i + 1) * C], xnT[:, 0],
                                       start=True, stop=True)
                    mm.then_inc(ring.filled(step, b), 1)
                elif name == "v":
                    ring.wait_free(pe, step, b)
                    for t in range(NT):
                        mm = pe.matmul(o[:, t * C:(t + 1) * C], xnT[:, 0, t * P:(t + 1) * P],
                                       w[:, W_QKV + 2 * C:W_QKV + 3 * C], start=True, stop=True)
                    mm.then_inc(ring.filled(step, b), 1)
                elif name == "k":
                    k0, width = KBANKS[step[1]]
                    pe.wait_ge(ctx_in.sem, ctx_in.now(b))
                    ring.wait_free(pe, step, b)
                    pe.matmul(o[:, 0:width], w[:, W_XK:W_XK + C], ctx_sb[:, k0:k0 + width],
                              start=True, stop=True).then_inc(ring.filled(step, b), 1)
                elif name == "vx":
                    ring.wait_free(pe, step, b)
                    for i, c in enumerate(VGROUPS[step[1]]):
                        rows = min(P, S - c * P)
                        mm = pe.matmul(o[0:rows, i * C:(i + 1) * C], ctx_sb[:, c * P:c * P + rows],
                                       w[:, W_XV:W_XV + C], start=True, stop=True)
                    mm.then_inc(ring.filled(step, b), 1)
                elif name == "score0":
                    pe.wait_ge(sqk_packed.sem, sqk_packed.now(b))
                    ring.wait_free(pe, step, b)
                    for t in range(NT):
                        mm = pe.matmul(o[:, t * T:(t + 1) * T], Qs[0:QK_ROWS, 0, 0, t * P:(t + 1) * P],
                                       Ks[0:QK_ROWS, 0, :], start=True, stop=True)
                    mm.then_inc(ring.filled(step, b), 1)
                elif name == "ff":
                    ring.wait_emptied(pe, "score0", b)
                    ring.wait_free(pe, step, b)
                    pe.matmul(o[:, 0:T], neg_before[:], S0[:, 0, :], start=True, stop=True)
                    pe.matmul(o[:, T:2 * T], neg_ones[:], S0[:, 0, :], start=True, stop=False)
                    pe.matmul(o[:, T:2 * T], neg_before[:], S0[:, 1, :], start=False,
                              stop=True).then_inc(ring.filled(step, b), 1)
                elif name == "biasT":
                    pe.wait_ge(bias_ready.sem, bias_ready.now(b))
                    ring.wait_free(pe, step, b)
                    pe.transpose(o[:, 0:P], bias[:, 0, 0:P], ident[:])
                    pe.transpose(o[:, P:2 * P], bias[:, 1, 0:P], ident[:])
                    pe.transpose(o[:, 2 * P:3 * P], bias[:, 1, P:T], ident[:]).then_inc(ring.filled(step, b), 1)
                elif name == "smax":
                    h = step[1]
                    ring.wait_free(pe, step, b)
                    q, k = Qs[0:QK_ROWS, h // 2, h % 2], Ks[0:QK_ROWS, h // 2]
                    pe.matmul(o[:, 0:P], q[:, 0:P], k[:, 0:P], start=True, stop=True)
                    pe.matmul(o[:, P:P + T], q[:, P:T], k, start=True, stop=True).then_inc(ring.filled(step, b), 1)
                elif name == "smT":
                    ring.wait_emptied(pe, ("smax", H - 1), b)
                    turn(step, smax, b)
                elif name == "sscore":
                    g, k = divmod(step[1], NT)
                    if step[1] == 0:
                        pe.wait_ge(ones_in, 32)
                        pe.wait_ge(sm_packed.sem, sm_packed.now(b))
                    wait_scores_taken(pe, step, b)
                    lo, width = (0, T) if k == 0 else (P, T - P)
                    for j in range(2):
                        mm = pe.matmul(p_sc[sc.at(step, b)][:, j, 0:2 * width], Ks[0:ALL_ROWS, 2 * g + j, k * P:(k + 1) * P],
                                       Qs[0:ALL_ROWS, 2 * g + j, :, lo:lo + width], start=True, stop=True)
                    mm.then_inc(sc.filled(step, b), 1)
                elif name == "ssum":
                    g = step[1]
                    ring.wait_free(pe, step, b)
                    ring.wait_emptied(pe, "v", b)
                    for k in range(NT):
                        job = ("sexp", NT * g + k)
                        pr.wait_filled(pe, job, b)
                        lo, width = (0, T) if k == 0 else (P, T - P)
                        mm = sums(o, Vs, pr.at(job, b), P, g, k, lo, width, k == 0, k == NT - 1)
                        if k < NT - 1:
                            mm.then_inc(pr.emptied(job, b), 1)
                    mm.then_inc(pr.emptied(job, b), 1)
                elif name in ("sy", "xy"):
                    t = step[1]
                    ring.wait_free(pe, step, b)
                    if name == "xy":
                        pe.wait_ge(sums_kept.sem, sums_kept.now(b))
                    else:
                        for g in range(G):
                            ring.wait_emptied(pe, ("ssum", g), b)
                    for g in range(G):
                        mm = pe.transpose(o[:, g * P:(g + 1) * P], yT[name[0]][:, g, t * P:(t + 1) * P], ident[:])
                    mm.then_inc(ring.filled(step, b), 1)
                elif name in ("sycT", "xycT"):
                    for t in range(NT):
                        ring.wait_emptied(pe, (name[0] + "y", t), b)
                    turn(step, yrow[name[0]], b)
                elif name in ("sproj", "xproj"):
                    ring.wait_emptied(pe, name[0] + "ycT", b)
                    ring.wait_free(pe, step, b)
                    w0 = W_PROJ if name == "sproj" else W_XO
                    for t in range(NT):
                        mm = pe.matmul(o[:, t * C:(t + 1) * C], ycT[name[0]][:, t * P:(t + 1) * P], w[:, w0:w0 + C],
                                       start=True, stop=True)
                    mm.then_inc(ring.filled(step, b), 1)
                elif name == "xn2T":
                    pe.wait_ge(xn_ready[1].sem, xn_ready[1].now(b))
                    turn(step, xn[:, 1], b)
                elif name == "q2":
                    ring.wait_emptied(pe, "xn2T", b)
                    ring.wait_free(pe, step, b)
                    pe.matmul(o[:, 0:T], w[:, W_XQ:W_XQ + C], xnT[:, 1], start=True,
                              stop=True).then_inc(ring.filled(step, b), 1)
                elif name == "xmax":
                    _, g, t, j, n = step
                    h = HG * g + j
                    k0, width = PIECES[n]
                    if (t, j, n) == (0, 0, 0):
                        if g == 0:
                            pe.wait_ge(q2_packed.sem, q2_packed.now(b))
                        pe.wait_ge(xk_packed[g].sem, xk_packed[g].now(b))
                    ring.wait_free(pe, step, b)
                    pe.matmul(o[:, 0:width], Qx[b % 2][0:QK_ROWS, h // 2, h % 2, t * P:(t + 1) * P],
                              Kx[0:QK_ROWS, h // 2, k0:k0 + width], start=True, stop=True).then_inc(ring.filled(step, b), 1)
                elif name == "xmT":
                    g = step[1]
                    pe.wait_ge(xmax_ready.sem, xmax_ready.now(b, g + 1))
                    turn(step, xmax[:, g % 2], b)
                elif name == "score":
                    _, g, c = step
                    rows = min(P, S - c * P)
                    if c == 0:
                        pe.wait_ge(xm_packed[g].sem, xm_packed[g].now(b))
                    wait_scores_taken(pe, step, b)
                    for j in range(2):
                        mm = pe.matmul(p_sc[sc.at(step, b)][0:rows, j, :], Kx[0:ALL_ROWS, 2 * g + j, c * P:c * P + rows],
                                       Qx[b % 2][0:ALL_ROWS, 2 * g + j, :, :], start=True, stop=True)
                    mm.then_inc(sc.filled(step, b), 1)
                elif name == "sum":
                    _, g, c = step
                    job = ("score", g, c)
                    if c == 0:
                        wait_past(pe, sums_kept.sem, sums_kept.now(b, g))
                        if g == 0:
                            ring.wait_emptied(pe, ("vx", 3), b)
                            for n in range(3):
                                ring.wait_emptied(pe, ("vx", n), b)
                    pr.wait_filled(pe, job, b)
                    mm = sums(p_pv, Vx[:, b % 2], pr.at(job, b), min(P, S - c * P), g, c, 0, T, c == 0, c == NC - 1)
                    mm.then_inc(pr.emptied(job, b), 1)
                elif name == "xn3T":
                    pe.wait_ge(xn_ready[2].sem, xn_ready[2].now(b))
                    turn(step, xn[:, 2], b)
                elif name == "router":
                    ring.wait_emptied(pe, "xn3T", b)
                    ring.wait_free(pe, step, b)
                    for t in range(NT):
                        mm = pe.matmul(o[:, t * E_RT:(t + 1) * E_RT], xnT[:, 2, t * P:(t + 1) * P],
                                       w[:, W_R:W_R + E_RT], start=True, stop=True)
                    mm.then_inc(ring.filled(step, b), 1)
                elif name == "gatesT":
                    pe.wait_ge(gates_ready.sem, gates_ready.now(b))
                    turn(step, gates, b)
                elif name == "h13":
                    n = step[1]
                    ring.wait_free(pe, step, b)
                    for i, w0 in enumerate((W_1, W_3)):
                        mm = pe.matmul(o[:, i * T:(i + 1) * T], w[:, w0 + n * P:w0 + (n + 1) * P], xnT[:, 2],
                                       start=True, stop=True)
                    mm.then_inc(ring.filled(step, b), 1)
                elif name == "gate":
                    n = step[1]
                    ring.wait_emptied(pe, "gatesT", b)
                    ring.wait_free(pe, step, b)
                    pe.matmul(o[:, 0:T], expert_rows[:, n, :], gatesT[:], start=True,
                              stop=True).then_inc(ring.filled(step, b), 1)
                elif name == "ffn":
                    for n in range(NB_RT):
                        ring.wait_emptied(pe, ("gate", n), b)
                    pe.wait_ge(h_ready.sem, h_ready.now(b))
                    ring.wait_free(pe, step, b)
                    for t in range(NT):
                        for n in range(NB):
                            mm = pe.matmul(o[:, t * C:(t + 1) * C], hT[:, n, t * P:(t + 1) * P],
                                           w[:, W_2 + n * P:W_2 + (n + 1) * P], start=(n == 0), stop=(n == NB - 1))
                    mm.then_inc(ring.filled(step, b), 1)

        @block.scalar
        def _(act):
            act.wait_ge(w_in, 48)
            act.wait_ge(colbs_ready, 1)

            def evacuate(dst, job, width, b, parts=P, **kw):
                ring.wait_filled(act, job, b)
                nc.scalar.activation(dst, p_r[ring.at(job, b)][0:parts, 0:width], kw.pop("func", ACT.Copy), **kw).then_inc(
                    ring.emptied(job, b), 1)

            for step, b in order:
                name = kind(step)
                if name in ("xn1T", "xn2T", "xn3T"):
                    evacuate(xnT[:, int(name[2]) - 1], step, T, b)
                elif name == "qk":
                    ring.wait_filled(act, step, b)
                    o = p_r[ring.at(step, b)]
                    nc.scalar.activation(qk[0][:, 0, :], o[:, 0:T], ACT.Identity, bias=colbs[:, B_Q:B_Q + 1], scale=SCALE)
                    nc.scalar.activation(qk[0][:, 1, :], o[:, T:2 * T], ACT.Identity,
                                         bias=colb[:, B_K:B_K + 1]).then_inc(ring.emptied(step, b), 1)
                elif name == "k":
                    k0, width = KBANKS[step[1]]
                    wait_past(act, kpart_ready.sem, kpart_ready.last(b))
                    evacuate(kf[:, k0:k0 + width], step, width, b, func=ACT.Identity, bias=colb[:, B_XK:B_XK + 1])
                elif name == "k_split" and step[1] in (0, 2):
                    if step[1] == 0:
                        for n in range(len(KBANKS)):
                            ring.wait_emptied(act, ("k", n), b)
                        wait_past(act, xk_written.sem, xk_written.last(b))
                    else:
                        act.wait_ge(kpart_step.sem, kpart_step.now(b, 2))
                    nc.scalar.activation(k_part[:, step[1] // 2, :], kf[:], ACT.Copy).then_inc(kpart_step.sem, 1)
                elif name == "biasT":
                    evacuate(biasT[:], step, 3 * P, b)
                elif name == "smT":
                    evacuate(sm_neg[:], step, T, b, parts=H, scale=-1.0)
                elif name == "sexp":
                    i = step[1]
                    width = T if i % NT == 0 else T - P
                    act.wait_ge(scores_added.sem, scores_added.now(b, i + 1))
                    pr.wait_free(act, step, b)
                    nc.scalar.activation(probs[:, pr.at(step, b), 0:HG * width], biased[:, i % 2, 0:HG * width],
                                         ACT.Exp).then_inc(pr.filled(step, b), 1)
                elif name == "ssum":
                    pr.wait_emptied(act, ("sexp", NT * step[1] + NT - 1), b)
                    nc.scalar.activation(yT["s"][:, step[1], :], p_r[ring.at(step, b)][:, 0:T],
                                         ACT.Copy).then_inc(ring.emptied(step, b), 1)
                elif name in ("sycT", "xycT"):
                    evacuate(ycT[name[0]][:], step, T, b)
                elif name == "q2":
                    evacuate(qk[1][:, 0, :], step, T, b, func=ACT.Identity, bias=colbs[:, B_XQ:B_XQ + 1], scale=SCALE)
                elif name == "xmT":
                    g = step[1]
                    if g or b:
                        act.wait_ge(xm_ready.sem, xm_ready.now(b, g))
                    evacuate(xm_neg[:], step, T, b, parts=HG, scale=-1.0)
                elif name == "score":
                    _, g, c = step
                    rows = min(P, S - c * P)
                    sc.wait_filled(act, step, b)
                    pr.wait_free(act, step, b)
                    nc.scalar.activation(probs[0:rows, pr.at(step, b), :],
                                         p_sc[sc.at(step, b)][0:rows].rearrange("p s n -> p (s n)"),
                                         ACT.Exp).then_inc(pr.filled(step, b), 1)
                elif name == "keep":
                    g = step[1]
                    pr.wait_emptied(act, ("score", g, NC - 1), b)
                    nc.scalar.activation(yT["x"][:, g, :], p_pv[:, 0:T], ACT.Copy).then_inc(sums_kept.sem, 1)
                elif name == "gate2":
                    for t in range(NT):
                        act.wait_ge(gate_step.sem, gate_step.now(b, 5))
                        nc.scalar.activation(eg[:, t, :], logits[:, t, 0:E_RT], ACT.Exp,
                                             bias=neg_best[:, t, :]).then_inc(eg_ready.sem, 1)
                elif name == "gatesT":
                    evacuate(gatesT[:], step, T, b, parts=E_RT)
                elif name == "h13":
                    n = step[1]
                    ring.wait_filled(act, step, b)
                    if n >= 2:
                        act.wait_ge(en1_ready.sem, en1_ready.now(b, n - 1))
                        act.wait_ge(h_ready.sem, h_ready.now(b, n - 1))
                    o = p_r[ring.at(step, b)]
                    nc.scalar.activation(en[:, n % 2, :], o[:, 0:T], ACT.Exp, scale=-1.0).then_inc(en_ready.sem, 1)
                    nc.scalar.activation(h13[:, n % 2].rearrange("p i n -> p (i n)"), o[:],
                                         ACT.Copy).then_inc(ring.emptied(step, b), 1)

        @block.vector
        def _(dve):
            nc.vector.memset(ones[:], 1.0).then_inc(ones_set, 1)
            nc.vector.memset(Qs[:].bitcast(F32), 0.0).then_inc(rows_set, 1)
            dve.wait_ge(w_in, 48)
            nc.vector.tensor_scalar(colbs[:], colb[:, 0:2], SCALE, None, ALU.mult).then_inc(colbs_ready, 1)
            dve.wait_ge(consts, 1)

            def heads_from(ps, r0, rows, m):
                return (ps[0:rows, 0:m * C].rearrange("p (t h d) -> p t h d", t=m, d=D),
                        rowb[0:rows, r0:r0 + C].rearrange("p (h d) -> p h d", d=D).unsqueeze(1).to_broadcast([rows, m, H, D]))

            for step, b in order:
                name = kind(step)
                o = p_r[ring.at(step, b)] if name in in_ring else None
                if name == "stats":
                    k = step[1]
                    src = (xin, x1, x2)[k]
                    s = ln_step[k]
                    if k == 0:
                        dve.wait_ge(x_in.sem, x_in.now(b))
                    else:
                        ring.wait_emptied(dve, ("sproj", "xproj")[k - 1], b)
                    for t in range(NT):
                        nc.vector.bn_stats(stats[:, k, t, :], src[:, t, :]).then_inc(s.sem, 1)
                    dve.wait_ge(s.sem, s.now(b, 2))
                    for t in range(NT):
                        nc.vector.bn_aggr(mv[:, k, t, :], stats[:, k, t, :]).then_inc(s.sem, 1)
                elif name == "norm":
                    k = step[1]
                    src = (xin, x1, x2)[k]
                    dve.wait_ge(ln_step[k].sem, ln_step[k].now(b))
                    dve.wait_ge(rstd_ready[k].sem, rstd_ready[k].now(b))
                    if b:
                        ring.wait_filled(dve, ("xn1T", "xn2T", "xn3T")[k], b - 1)
                    for t in range(NT):
                        nc.vector.tensor_scalar(xn[:, k, t, :], src[:, t, :], mv[:, k, t, 0:1], rstd[:, k, t, :],
                                                ALU.subtract, ALU.mult).then_inc(xn_ready[k].sem, 1)
                elif name == "split":
                    _, k, i = step
                    s = part_step[k]
                    if i == 0:
                        ring.wait_emptied(dve, ("qk", "q2")[k], b)
                        written = (sqk_written, q2_written)[k]
                        wait_past(dve, written.sem, written.last(b))
                        nc.vector.tensor_copy(qk_part[k][:, 0], qk[k][:]).then_inc(s.sem, 1)
                        continue
                    dve.wait_ge(s.sem, s.now(b, i))
                    if i == 1:
                        nc.vector.tensor_tensor(qk[k][:], qk[k][:], qk_part[k][:, 0], ALU.subtract).then_inc(s.sem, 1)
                    elif i == 2:
                        nc.vector.tensor_copy(qk_part[k][:, 1], qk[k][:]).then_inc(s.sem, 1)
                    else:
                        nc.vector.tensor_tensor(qk_part[k][:, 2], qk[k][:], qk_part[k][:, 1],
                                                ALU.subtract).then_inc(part_ready[k].sem, 1)
                        if k == 0 and b == 0:
                            for q in Qx:
                                nc.vector.memset(q[:].bitcast(F32), 0.0).then_inc(rows_set, 1)
                elif name == "v":
                    ring.wait_filled(dve, step, b)
                    if b:
                        ring.wait_emptied(dve, ("ssum", G - 1), b - 1)
                    v, r = heads_from(o, R_V, P, NT)
                    nc.vector.tensor_tensor(Vs[:, 0:NT * VROW].rearrange("p (t h d) -> p t h d", t=NT, d=VH)[:, :, :, 0:D],
                                            v, r, ALU.add).then_inc(ring.emptied(step, b), 1)
                elif name == "vx":
                    chunks = VGROUPS[step[1]]
                    m, rows, c0 = len(chunks), min(P, S - chunks[-1] * P), chunks[0]
                    ring.wait_filled(dve, step, b)
                    if b > 1:
                        pr.wait_emptied(dve, ("score", G - 1, NC - 1), b - 2)
                    v, r = heads_from(o, R_XV, rows, m)
                    dst = Vx[0:rows, b % 2, c0 * VROW:(c0 + m) * VROW].rearrange("p (t h d) -> p t h d", t=m, d=VH)
                    nc.vector.tensor_tensor(dst[:, :, :, 0:D], v, r, ALU.add).then_inc(ring.emptied(step, b), 1)
                elif name == "score0":
                    ring.wait_filled(dve, step, b)
                    nc.vector.scalar_tensor_tensor(out=S0[:], in0=o[:].rearrange("p (t n) -> p t n", t=NT),
                                                   scalar=0.0, in1=earlier[:], op0=ALU.max,
                                                   op1=ALU.mult).then_inc(ring.emptied(step, b), 1)
                elif name == "ff":
                    ring.wait_filled(dve, step, b)
                    nc.vector.tensor_tensor(nff[:, :, 0:T], o[:].rearrange("p (t n) -> p t n", t=NT), acausal[:],
                                            ALU.add).then_inc(ring.emptied(step, b), 1)
                elif name == "top":
                    r = step[1]
                    if r == 0:
                        ring.wait_emptied(dve, "ff", b)
                    for t in range(NT):
                        src = nff[:, t, :] if r == 0 else top[:, (r - 1) % 2, t, :]
                        if r:
                            dve.wait_ge(top_step.sem, top_step.now(b, 4 * r - 1 + t))
                        nc.vector.max(top8[:, t, :], src).then_inc(top_step.sem, 1)
                    for t in range(NT):
                        src = nff[:, t, :] if r == 0 else top[:, (r - 1) % 2, t, :]
                        dve.wait_ge(top_step.sem, top_step.now(b, 4 * r + t + 1))
                        nc.vector.match_replace(top[:, r % 2, t, :], top8[:, t, :], src, TAKEN).then_inc(top_step.sem, 1)
                elif name == "drop":
                    dve.wait_ge(top_step.sem, top_step.now(b))
                    nc.vector.scalar_tensor_tensor(out=S0[:], in0=top[:, (ROUNDS - 1) % 2, :, 0:T], scalar=TAKEN_BELOW,
                                                   in1=off_diag[:], op0=ALU.is_gt, op1=ALU.mult).then_inc(drop_ready.sem, 1)
                elif name == "bias":
                    dve.wait_ge(drop_ready.sem, drop_ready.now(b))
                    nc.vector.tensor_tensor(bias[:], S0[:], nff[:, :, 0:T], ALU.add).then_inc(bias_ready.sem, 1)
                elif name == "smax":
                    h = step[1]
                    ring.wait_filled(dve, step, b)
                    if h == 0:
                        dve.wait_ge(bias_ready.sem, bias_ready.now(b))
                    if h >= 2:
                        ring.wait_emptied(dve, ("smax", h - 2), b)
                    elif b:
                        ring.wait_emptied(dve, ("smax", H - 2 + h), b - 1)
                    elif h == 0:
                        dve.wait_ge(ones_in, 32)
                    nc.vector.tensor_tensor_reduce(junk[:, h % 2, 0, 0:P], o[:, 0:P], bias[:, 0, 0:P], 1.0, TAKEN, ALU.add,
                                                   ALU.max, smax[:, 0, h:h + 1]).then_inc(smax_first.sem, 1)
                    nc.vector.tensor_tensor_reduce(junk[:, h % 2, 1, :], o[:, P:P + T], bias[:, 1, :], 1.0, TAKEN, ALU.add,
                                                   ALU.max, smax[:, 1, h:h + 1]).then_inc(ring.emptied(step, b), 1)
                elif name == "sscore":
                    i = step[1]
                    k = i % NT
                    width = T if k == 0 else T - P
                    sc.wait_filled(dve, step, b)
                    if i == 0:
                        ring.wait_emptied(dve, "biasT", b)
                    if i >= 2:
                        pr.wait_filled(dve, ("sexp", i - 2), b)
                    elif b:
                        pr.wait_filled(dve, ("sexp", G * NT - 2 + i), b - 1)
                    four = [P, 2, 2, width]
                    nc.vector.tensor_tensor(biased[:, i % 2, 0:HG * width].rearrange("p (s q n) -> p s q n", s=2, q=2),
                                            p_sc[sc.at(step, b)][:, :, 0:2 * width].rearrange("p s (q n) -> p s q n", q=2),
                                            biasT[:, k * T:k * T + width].unsqueeze(1).unsqueeze(1).to_broadcast(four),
                                            ALU.add).then_inc(scores_added.sem, 1)
                elif name in ("sy", "xy"):
                    t, k = step[1], name[0]
                    ring.wait_filled(dve, step, b)
                    v = o[:].rearrange("p (h c) -> p h c", c=32)
                    nc.vector.reciprocal(rden[k][:, t, :], v[:, :, D]).then_inc(rden_ready[k].sem, 1)
                    dve.wait_ge(rden_ready[k].sem, rden_ready[k].now(b, t + 1))
                    nc.vector.tensor_tensor(yrow[k][:, t, :].rearrange("p (h d) -> p h d", d=D), v[:, :, 0:D],
                                            rden[k][:, t, :].unsqueeze(2).to_broadcast([P, H, D]),
                                            ALU.mult).then_inc(ring.emptied(step, b), 1)
                elif name == "sproj":
                    ring.wait_filled(dve, step, b)
                    dve.wait_ge(xb_ready.sem, xb_ready.now(b))
                    if b:
                        dve.wait_ge(x1b_ready.sem, x1b_ready.last(b))
                    nc.vector.tensor_tensor(x1[:], o[:, 0:NT * C].rearrange("p (t c) -> p t c", t=NT), xb[:],
                                            ALU.add).then_inc(ring.emptied(step, b), 1)
                elif name == "xmax":
                    _, g, t, j, n = step
                    ring.wait_filled(dve, step, b)
                    nc.vector.tensor_reduce(xmax4[:, g % 2, t, j, n:n + 1], o[:, 0:PIECES[n][1]], AX.X,
                                            ALU.max).then_inc(ring.emptied(step, b), 1)
                elif name == "xmax8":
                    g = step[1]
                    ring.wait_emptied(dve, ("xmax", g, NT - 1, HG - 1, 3), b)
                    nc.vector.tensor_reduce(xmax[:, g % 2], xmax4[:, g % 2], AX.X, ALU.max).then_inc(xmax_ready.sem, 1)
                elif name == "xproj":
                    ring.wait_filled(dve, step, b)
                    dve.wait_ge(x1b_ready.sem, x1b_ready.now(b))
                    nc.vector.tensor_tensor(x2[:], o[:, 0:NT * C].rearrange("p (t c) -> p t c", t=NT), x1b[:, b % 2],
                                            ALU.add).then_inc(ring.emptied(step, b), 1)
                elif name == "router":
                    ring.wait_filled(dve, step, b)
                    nc.vector.tensor_tensor(logits[:, :, 0:E_RT], o[:, 0:NT * E_RT].rearrange("p (t e) -> p t e", t=NT),
                                            rowb[:, R_R:R_R + E_RT].unsqueeze(1).to_broadcast([P, NT, E_RT]),
                                            ALU.add).then_inc(ring.emptied(step, b), 1)
                elif name == "gate1":
                    s = gate_step
                    ring.wait_emptied(dve, "router", b)
                    for t in range(NT):
                        nc.vector.max(best8[:, t, :], logits[:, t, :]).then_inc(s.sem, 1)
                    dve.wait_ge(s.sem, s.now(b, 2))
                    for t in range(NT):
                        nc.vector.match_replace(ranked[:, t, :], best8[:, t, :], logits[:, t, :], TAKEN).then_inc(s.sem, 1)
                    nc.vector.tensor_scalar(neg_best[:], best8[:, :, GDUMMY:GDUMMY + 1], -1.0, None, ALU.mult).then_inc(s.sem, 1)
                elif name == "gate3":
                    s = gate_step
                    dve.wait_ge(eg_ready.sem, eg_ready.now(b))
                    dve.wait_ge(s.sem, s.now(b, 5))
                    nc.vector.scalar_tensor_tensor(out=egm[:], in0=ranked[:, :, 0:E_RT], scalar=TAKEN_BELOW, in1=eg[:],
                                                   op0=ALU.is_lt, op1=ALU.mult).then_inc(s.sem, 1)
                    dve.wait_ge(s.sem, s.now(b, 6))
                    nc.vector.tensor_reduce(gsum[:], egm[:], AX.X, ALU.add).then_inc(s.sem, 1)
                    dve.wait_ge(s.sem, s.now(b, 7))
                    nc.vector.reciprocal(grec[:], gsum[:]).then_inc(s.sem, 1)
                    dve.wait_ge(s.sem, s.now(b, 8))
                    nc.vector.tensor_tensor(gates[:], egm[:], grec[:].to_broadcast([P, NT, E_RT]),
                                            ALU.mult).then_inc(gates_ready.sem, 1)
                elif name == "h":
                    n = step[1]
                    k = n % 2
                    dve.wait_ge(en1_ready.sem, en1_ready.now(b, n + 1))
                    if n >= 2:
                        ring.wait_emptied(dve, ("gate", n - 2), b)
                    nc.vector.reciprocal(sg[:, k, :], en[:, k, :]).then_inc(rec_ready.sem, 1)
                elif name == "gate":
                    n = step[1]
                    ring.wait_filled(dve, step, b)
                    dve.wait_ge(h_ready.sem, h_ready.now(b, n + 1))
                    nc.vector.tensor_tensor(hT[:, n, :], o[:, 0:T], sg[:, n % 2, :],
                                            ALU.mult).then_inc(ring.emptied(step, b), 1)
                elif name == "ffn":
                    ring.wait_filled(dve, step, b)
                    wait_past(dve, stored.sem, stored.last(b))
                    nc.vector.tensor_tensor(xout[:], o[:, 0:NT * C].rearrange("p (t c) -> p t c", t=NT), x2[:],
                                            ALU.add).then_inc(ring.emptied(step, b), 1)


def kernel(x, ctx_1024, L0_attn_w_attn, L0_attn_b_attn, L0_attn_w_proj, L0_attn_b_proj, L0_xattn_Wq, L0_xattn_bq,
           L0_xattn_Wk, L0_xattn_bk, L0_xattn_Wv, L0_xattn_bv, L0_xattn_Wo, L0_xattn_bo, L0_ffn_router_w,
           L0_ffn_router_b, L0_ffn_routed_w1, L0_ffn_routed_w3, L0_ffn_routed_w2, L0_ffn_shared_w1,
           L0_ffn_shared_w3, L0_ffn_shared_w2):
    import concourse.bacc as bacc
    from concourse.bass_utils import run_bass_kernel_spmd

    def wide(routed, shared):
        both = np.concatenate([np.asarray(routed), np.asarray(shared)], 0)
        return both.transpose(1, 0, 2).reshape(C, -1)

    w2 = np.concatenate([np.asarray(L0_ffn_routed_w2), np.asarray(L0_ffn_shared_w2)], 0)
    w2 = w2.reshape(NB, P, C).transpose(1, 0, 2).reshape(P, NB * C)
    b_attn = np.asarray(L0_attn_b_attn)
    arrays = {
        "x": np.asarray(x),
        "ctxT": np.asarray(ctx_1024).transpose(0, 2, 1),
        "w_all": np.concatenate([np.asarray(L0_attn_w_attn).T, np.asarray(L0_attn_w_proj).T, np.asarray(L0_xattn_Wq).T,
                                 np.asarray(L0_xattn_Wk).T, np.asarray(L0_xattn_Wv).T, np.asarray(L0_xattn_Wo).T,
                                 np.asarray(L0_ffn_router_w), wide(L0_ffn_routed_w1, L0_ffn_shared_w1),
                                 wide(L0_ffn_routed_w3, L0_ffn_shared_w3), w2], 1),
        "col_bias": np.stack([b_attn[0:C], np.asarray(L0_xattn_bq), b_attn[C:2 * C], np.asarray(L0_xattn_bk)], 1),
        "row_bias": np.concatenate([b_attn[2 * C:], np.asarray(L0_attn_b_proj), np.asarray(L0_xattn_bv),
                                    np.asarray(L0_xattn_bo), np.asarray(L0_ffn_router_b)])[None],
    }
    nc = bacc.Bacc("TRN2", target_bir_lowering=False, num_devices=1)
    arrays = {f"in_{k}": np.ascontiguousarray(v) for k, v in arrays.items()}
    args = [nc.dram_tensor(k, v.shape, mybir.dt.from_np(v.dtype), kind="ExternalInput").ap() for k, v in arrays.items()]
    args.append(nc.dram_tensor("out_x", (B, T, C), F32, kind="ExternalOutput").ap())
    build(nc, *args)
    return run_bass_kernel_spmd(nc, [arrays], core_ids=[0]).results[0]["out_x"]
```
